# Optimizing a Trainium2 kernel written in Bass

```python
import numpy as np
import jax
import jax.numpy as jnp

def _softmax(x, axis=-1):
    return jax.nn.softmax(x, axis=axis)

def _gelu(x):
    return jax.nn.gelu(x, approximate=True)

def _silu(x):
    return jax.nn.silu(x)

def _sigmoid(x):
    return jax.nn.sigmoid(x)

def _layernorm(x, axis=-1, eps=1e-05):
    m = jnp.mean(x, axis=axis, keepdims=True)
    v = jnp.var(x, axis=axis, keepdims=True)
    return (x - m) / jnp.sqrt(v + eps)

def _scatter_add(tgt, idx, src, axis=0):
    return tgt.at[idx].add(src)

def _segment_sum(src, seg, n):
    return jax.ops.segment_sum(src, seg, n)
kernel_name = 'mk_hybrid_d1_jaxref_r8_a32d94'

def setup_inputs(seed: int=0):
    np.random.seed(seed)
    _w = jnp.asarray

    def _L0_attn_a_setup():
        import jax, jax.numpy as jnp
        import numpy as np
        import math
        B, S, DM, H = (4, 512, 128, 16)
        HD = DM // H
        key = jax.random.key(seed)
        ks = jax.random.split(key, 5)

        def xavier(k, shape):
            bound = math.sqrt(6.0 / (shape[0] + shape[1]))
            return jax.random.uniform(k, shape, jnp.float32, -bound, bound)
        return {'x': jax.random.normal(ks[0], (B, S, DM), jnp.float32), 'Wq': xavier(ks[1], (DM, DM)), 'Wk': xavier(ks[2], (DM, DM)), 'Wv': xavier(ks[3], (DM, DM)), 'Wfc': xavier(ks[4], (DM, DM))}
    _L0_attn_a_in = _L0_attn_a_setup()

    def _L0_attn_b_setup():
        import jax, jax.numpy as jnp
        import numpy as np
        D_MODEL = 128
        N_HEADS = 16
        HEAD_DIM = D_MODEL // N_HEADS
        BUCKET = 64
        key = jax.random.key(seed)
        k1, k2, k3 = jax.random.split(key, 3)
        B, T = (4, 512)
        x = jax.random.normal(k1, (B, T, D_MODEL), dtype=jnp.float32)
        W_qkv = jax.random.normal(k2, (3 * D_MODEL, D_MODEL), dtype=jnp.float32) * D_MODEL ** (-0.5)
        W_out = jax.random.normal(k3, (D_MODEL, D_MODEL), dtype=jnp.float32) * D_MODEL ** (-0.5)
        return {'x': x, 'W_qkv': W_qkv, 'W_out': W_out}
    _L0_attn_b_in = _L0_attn_b_setup()

    def _L0_ffn_setup():
        import jax, jax.numpy as jnp
        import numpy as np
        B, T, DIM, H, DH, TOPK = (4, 256, 128, 8, 64, 3)
        key = jax.random.key(seed)
        ks = jax.random.split(key, 6)
        x = jax.random.normal(ks[0], (B, T, DIM), dtype=jnp.float32)
        sc = 1.0 / np.sqrt(DIM)
        Wq = jax.random.normal(ks[1], (DIM, H * DH), dtype=jnp.float32) * sc
        Wkv = jax.random.normal(ks[2], (DIM, 2 * H * DH), dtype=jnp.float32) * sc
        Ws = jax.random.normal(ks[3], (DIM, H), dtype=jnp.float32) * sc
        Wo = jax.random.normal(ks[4], (H, DH, DIM), dtype=jnp.float32) * (1.0 / np.sqrt(DH))
        bo = jax.random.normal(ks[5], (H, DIM), dtype=jnp.float32) * 0.01
        return {'x': x, 'Wq': Wq, 'Wkv': Wkv, 'Ws': Ws, 'Wo': Wo, 'bo': bo}
    _L0_ffn_in = _L0_ffn_setup()
    _d = {'L0_attn_a_x': _L0_attn_a_in['x'], 'L0_attn_a_Wq': _L0_attn_a_in['Wq'], 'L0_attn_a_Wk': _L0_attn_a_in['Wk'], 'L0_attn_a_Wv': _L0_attn_a_in['Wv'], 'L0_attn_a_Wfc': _L0_attn_a_in['Wfc'], 'L0_attn_b_W_qkv': _L0_attn_b_in['W_qkv'], 'L0_attn_b_W_out': _L0_attn_b_in['W_out'], 'L0_ffn_Wq': _L0_ffn_in['Wq'], 'L0_ffn_Wkv': _L0_ffn_in['Wkv'], 'L0_ffn_Ws': _L0_ffn_in['Ws'], 'L0_ffn_Wo': _L0_ffn_in['Wo'], 'L0_ffn_bo': _L0_ffn_in['bo']}
    _x0 = _d['L0_attn_a_x']
    _d['L0_attn_a_x'] = jax.random.normal(jax.random.fold_in(jax.random.key(seed), 1), (8, 512, 128), dtype=_x0.dtype)
    del _x0
    return _d

def reference(L0_attn_a_x, L0_attn_a_Wq, L0_attn_a_Wk, L0_attn_a_Wv, L0_attn_a_Wfc, L0_attn_b_W_qkv, L0_attn_b_W_out, L0_ffn_Wq, L0_ffn_Wkv, L0_ffn_Ws, L0_ffn_Wo, L0_ffn_bo):

    def _L0_attn_a_ref(x, Wq, Wk, Wv, Wfc):
        import jax, jax.numpy as jnp
        import numpy as np
        import math
        B, S, DM, H = (4, 512, 128, 16)
        HD = DM // H
        b, s, dm = x.shape
        h, hd = (H, dm // H)
        Q = (x @ Wq.T).reshape(b, s, h, hd)
        K = (x @ Wk.T).reshape(b, s, h, hd)
        V = (x @ Wv.T).reshape(b, s, h, hd)
        scores = jnp.einsum('bshd,bstd->bsht', Q, K) / math.sqrt(hd)
        attn = jax.nn.softmax(scores, axis=-1)
        out = jnp.einsum('bsht,bstd->bshd', attn, V).reshape(b, s, dm)
        return out @ Wfc.T

    def _L0_attn_b_ref(x, W_qkv, W_out):
        import jax, jax.numpy as jnp
        import numpy as np
        D_MODEL = 128
        N_HEADS = 16
        HEAD_DIM = D_MODEL // N_HEADS
        BUCKET = 64
        B, T, _ = x.shape
        qkv = x @ W_qkv.T
        qkv = qkv.reshape(B, T, 3 * N_HEADS, HEAD_DIM).transpose(0, 2, 1, 3)
        q, k, v = jnp.split(qkv, 3, axis=1)
        q = jax.nn.softmax(q, axis=-1) * HEAD_DIM ** (-0.5)
        k = jnp.exp(k)
        n = T // BUCKET
        bucket = lambda t: t.reshape(B, N_HEADS, n, BUCKET, HEAD_DIM)
        b_q, b_k, b_v = (bucket(q), bucket(k), bucket(v))
        b_k_sum = jnp.sum(b_k, axis=-2)
        b_k_cumsum = jnp.cumsum(b_k_sum, axis=-2)
        b_k_cumsum = jnp.pad(b_k_cumsum, ((0, 0), (0, 0), (1, 0), (0, 0)))[:, :, :-1]
        context = jnp.einsum('bhnsd,bhnse->bhnde', b_k, b_v)
        context = jnp.cumsum(context, axis=-3)
        context = jnp.pad(context, ((0, 0), (0, 0), (1, 0), (0, 0), (0, 0)))[:, :, :-1]
        den = jnp.einsum('bhnsd,bhnd->bhns', b_q, b_k_cumsum)
        D_inv = 1.0 / jnp.maximum(den, 1e-06)
        attn = jnp.einsum('bhnsd,bhnde,bhns->bhnse', b_q, context, D_inv)
        xo = attn.reshape(B, N_HEADS, T, HEAD_DIM)
        xo = xo.transpose(0, 2, 1, 3).reshape(B, T, D_MODEL)
        return xo @ W_out.T

    def _L0_ffn_ref(x, Wq, Wkv, Ws, Wo, bo):
        import jax, jax.numpy as jnp
        import numpy as np
        B, T, DIM, H, DH, TOPK = (4, 256, 128, 8, 64, 3)
        b, t, _ = x.shape
        s = jax.nn.sigmoid(x @ Ws)
        vals, idx = jax.lax.top_k(s, TOPK)
        bi = jnp.arange(b)[:, None, None]
        ti = jnp.arange(t)[None, :, None]
        scores = jnp.zeros_like(s).at[bi, ti, idx].set(vals)
        q = (x @ Wq).reshape(b, t, H, DH).transpose(0, 2, 1, 3)
        kv = (x @ Wkv).reshape(b, t, 2, H, DH).transpose(2, 0, 3, 1, 4)
        k, v = (kv[0], kv[1])
        scale = DH ** (-0.5)
        attn = jax.nn.softmax(jnp.einsum('bhid,bhjd->bhij', q * scale, k), axis=-1)
        out = jnp.einsum('bhij,bhjd->bhid', attn, v)
        proj = jnp.einsum('bhtd,hde->bhte', out, Wo) + bo[None, :, None, :]
        return jnp.einsum('bhte,bth->bte', proj, scores)
    x = L0_attn_a_x
    x = x + _L0_attn_a_ref(_layernorm(x, axis=-1), L0_attn_a_Wq, L0_attn_a_Wk, L0_attn_a_Wv, L0_attn_a_Wfc)
    x = x + _L0_ffn_ref(_layernorm(x, axis=-1), L0_ffn_Wq, L0_ffn_Wkv, L0_ffn_Ws, L0_ffn_Wo, L0_ffn_bo)
    x = x + _L0_attn_b_ref(_layernorm(x, axis=-1), L0_attn_b_W_qkv, L0_attn_b_W_out)
    x = x + _L0_ffn_ref(_layernorm(x, axis=-1), L0_ffn_Wq, L0_ffn_Wkv, L0_ffn_Ws, L0_ffn_Wo, L0_ffn_bo)
    return x

_drawn_inputs = setup_inputs


def setup_inputs(seed=0):
    import zlib

    import numpy as np

    out = dict(_drawn_inputs(seed))
    spreads = {}
    factors = {}
    for name, (base, spread) in spreads.items():
        noise = np.random.default_rng([zlib.crc32(name.encode()), seed]).standard_normal(out[name].shape)
        drawn = base * np.exp(spread * noise) if base else spread * noise
        out[name] = jnp.asarray(drawn.astype(out[name].dtype))
    for name, factor in factors.items():
        out[name] = (out[name] * factor).astype(out[name].dtype)
    return out
```

```python
import concourse.bass as bass
from concourse import mybir
from contextlib import ExitStack


def bass_hybrid_attention_ffn_kernel(
    nc: bass.Bass,
    x_in: bass.AP,
    a_wq: bass.AP,
    a_wk: bass.AP,
    a_wv: bass.AP,
    a_wfc: bass.AP,
    b_wqkv: bass.AP,
    b_wout: bass.AP,
    f_wq: bass.AP,
    f_wkv: bass.AP,
    f_ws: bass.AP,
    f_wo: bass.AP,
    f_bo: bass.AP,
    out: bass.AP,
):
    fp32 = mybir.dt.float32
    fp32r = mybir.dt.float32r
    ALU = mybir.AluOpType
    ACT = mybir.ActivationFunctionType
    AX = mybir.AxisListType

    B, T, C = x_in.shape
    P = 128
    NT = T // P
    AH = 16
    AD = C // AH
    FH = f_bo.shape[0]
    FD = f_wo.shape[1]
    FC = FH * FD
    NP = FH // 2
    TOPK = 3
    EPS = 1e-5
    BUCKET = 64
    NB = T // BUCKET
    CW = C + AH
    UNITS = FH * NT
    A_SCALE = float(AD) ** -0.5
    F_SCALE = float(FD) ** -0.5
    PERIODS = 2 * B
    A_AHEAD = 2
    B_FROM = B - A_AHEAD

    ctx = ExitStack()
    with ctx:
        def sb(name, shape, dt=fp32):
            return ctx.enter_context(nc.sbuf_tensor(name, shape, dt))

        def sem(name):
            return ctx.enter_context(nc.semaphore(name))

        x_all = sb("x_all", [P, 2 * B, NT * C])
        ident = sb("ident", [P, P])
        ctx_mask = sb("ctx_mask", [P, CW])
        before = sb("before", [P, FH, FH])
        after = sb("after", [P, FH, FH])
        minus_half = sb("minus_half", [P, NT])
        a_w = sb("a_w", [P, 3 * C])
        a_fc = sb("a_fc", [P, C])
        b_w = sb("b_w", [P, 3 * C])
        b_out = sb("b_out", [P, C])
        raw_ws = sb("raw_ws", [P, FH])
        w_hi = sb("w_hi", [P, 3 * FC], fp32r)
        w_lo = sb("w_lo", [P, 3 * FC], fp32r)
        ws_hi = sb("ws_hi", [P, FH], fp32r)
        ws_lo = sb("ws_lo", [P, FH], fp32r)
        wo = sb("wo", [P, NP, C])
        bo = sb("bo", [FH, C])

        f_stats = sb("f_stats", [P, NT, 6])
        f_mv = sb("f_mv", [P, NT, 2])
        f_var = sb("f_var", [P, NT])
        f_rstd = sb("f_rstd", [P, NT])
        f_xn = sb("f_xn", [P, NT, C])
        xt_hi = sb("xt_hi", [P, T], fp32r)
        xt_lo = sb("xt_lo", [P, T], fp32r)
        q_both = sb("q_both", [P, 2, 2, T], fp32r)
        k_hi = sb("k_hi", [P, 2, T], fp32r)
        k_cross = sb("k_cross", [P, 2, 2, T], fp32r)
        v_sb = sb("v_sb", [P, NT, FC])
        neg_max = sb("neg_max", [P, UNITS])
        row_sum = sb("row_sum", [P, UNITS])
        probs = sb("probs", [P, 4, T])
        probs_t = sb("probs_t", [P, 4, NT, T])
        recip = sb("recip", [P, 2, NT])
        scale_w = sb("scale_w", [P, NT, 2, FD])
        scale_t = sb("scale_t", [P, T])
        out_t = sb("out_t", [P, NP, T])
        raw_wq = probs_t[:, 0, 0, :]
        raw_wkv = probs_t[:, 0, 1:3, :].rearrange("p a c -> p (a c)")
        raw_sq = out_t[:, 0:2, :].rearrange("p a (k c) -> p (a k) c", c=C)
        g_exp = sb("g_exp", [P, NT, FH])
        g_den = sb("g_den", [P, NT, FH])
        g_sig = sb("g_sig", [P, NT, FH])
        g_gt = sb("g_gt", [P, NT, FH, FH])
        g_ge = sb("g_ge", [P, NT, FH, FH])
        g_rank = sb("g_rank", [P, NT, FH])
        gate = sb("gate", [P, NT, FH])
        gate_t = sb("gate_t", [FH, T])

        s_stats = sb("s_stats", [P, NT, 6])
        s_mv = sb("s_mv", [P, NT, 2])
        s_var = sb("s_var", [P, NT])
        s_rstd = sb("s_rstd", [P, NT])
        s_xn = sb("s_xn", [P, NT, C])
        s_xt = sb("s_xt", [P, T])
        s_qkv = sb("s_qkv", [P, NT, 3 * C + AH])
        s_ot = sb("s_ot", [P, T])
        s_o = sb("s_o", [P, NT, C])
        a_prod = sb("a_prod", [P, 2, AH * AH * AD])
        a_s = sb("a_s", [P, NT * AH, AH])
        a_p = sb("a_p", [P, NT * AH, AH])
        a_max = sb("a_max", [P, NT * AH])
        a_sum = sb("a_sum", [P, NT * AH])
        a_rec = sb("a_rec", [P, NT * AH])
        b_q = sb("b_q", [P, NT, C])
        b_e = sb("b_e", [P, NT, C])
        b_k = sb("b_k", [P, 2, NT, C])
        b_cum = a_prod[:, :, :].rearrange("p a n -> p (a n)")[:, 0:NB * CW].rearrange("p (n c) -> p n c", c=CW)
        b_ctx = sb("b_ctx", [P, NB, CW])
        b_qt = sb("b_qt", [P, T])
        b_den = sb("b_den", [P, 2, AH])
        b_inv = sb("b_inv", [P, 2, AH])

        def bank(name):
            return ctx.enter_context(nc.psum_tensor(name, [P, 512], fp32))

        scores = [bank(f"scores{i}") for i in range(3)]
        turned = [bank(f"turned{i}") for i in range(2)]
        heads_out = bank("heads_out")
        misc = bank("misc")
        side = bank("side")

        loaded_x = sem("loaded_x")
        loaded_w = sem("loaded_w")
        loaded_f = sem("loaded_f")
        ident_done = sem("ident_done")
        masks_done = sem("masks_done")
        ones_done = sem("ones_done")
        w_turned = sem("w_turned")
        w_copied = sem("w_copied")
        w_hi_done = sem("w_hi_done")
        w_lo_done = sem("w_lo_done")
        f_chain = sem("f_chain")
        s_chain = sem("s_chain")
        p_chain = sem("p_chain")
        f_var_ready = sem("f_var_ready")
        f_rstd_ready = sem("f_rstd_ready")
        f_xn_ready = sem("f_xn_ready")
        xt_hi_ready = sem("xt_hi_ready")
        xt_lo_ready = sem("xt_lo_ready")
        qk_hi_ready = sem("qk_hi_ready")
        qk_lo_ready = sem("qk_lo_ready")
        v_ready = sem("v_ready")
        misc_full = sem("misc_full")
        scores_ready = sem("scores_ready")
        max_ready = sem("max_ready")
        exp_done = sem("exp_done")
        turned_ready = sem("turned_ready")
        turned_by_act = sem("turned_by_act")
        turned_by_dve = sem("turned_by_dve")
        heads_ready = sem("heads_ready")
        heads_scaled = sem("heads_scaled")
        recip_ready = sem("recip_ready")
        scale_ready = sem("scale_ready")
        scale_t_ready = sem("scale_t_ready")
        gate_exp_ready = sem("gate_exp_ready")
        gate_ready = sem("gate_ready")
        gate_t_ready = sem("gate_t_ready")
        f_x_done = sem("f_x_done")
        side_full = sem("side_full")
        s_var_ready = sem("s_var_ready")
        s_rstd_ready = sem("s_rstd_ready")
        s_xn_ready = sem("s_xn_ready")
        s_xt_ready = sem("s_xt_ready")
        s_qkv_ready = sem("s_qkv_ready")
        s_o_ready = sem("s_o_ready")
        s_ot_ready = sem("s_ot_ready")
        a_prod_ready = sem("a_prod_ready")
        a_prod_used = sem("a_prod_used")
        a_s_ready = sem("a_s_ready")
        a_p_ready = sem("a_p_ready")
        a_x_done = sem("a_x_done")
        b_q_ready = sem("b_q_ready")
        b_e_ready = sem("b_e_ready")
        b_k_ready = sem("b_k_ready")
        b_qn_ready = sem("b_qn_ready")
        b_qt_ready = sem("b_qt_ready")
        b_cum_ready = sem("b_cum_ready")
        b_ctx_ready = sem("b_ctx_ready")
        b_x_done = sem("b_x_done")
        stored = sem("stored")

        PAIR = 2 * NT
        LAST = PERIODS - 1
        MISC_SLOTS = {0: "q1", 1: "k1", 2: "scale3-", 3: "logits", 5: "v0", 6: "v1", 7: "v2", 8: "q2", 9: "k2",
                      10: "v3", 11: "scale0", 13: "gate_t", 16: "q3", 17: "k3", 19: "scale1", 21: "xt+",
                      24: "q0+", 25: "k0+", 27: "scale2"}
        PV_SLOTS = {PAIR * p + 1 + c: (f"{p - 1}" if p else f"{NP - 1}-", c) for p in range(NP) for c in range(NT)}
        RECIP_SLOTS = {PAIR * p: (f"{p - 1}" if p else f"{NP - 1}-") for p in range(NP)}
        OUT_SLOTS = {PAIR * p + PAIR - 3: (f"{p - 1}" if p else f"{NP - 1}-") for p in range(NP)}
        WO_SLOTS = {9 + t: t for t in range(NT)}
        NORM_SLOT, XN_SLOT = 16, 19

        def runs(phase, task):
            if phase == "start":
                return task[-1] == "+"
            return not (phase == "first" and task[-1] == "-" or phase == "last" and task[-1] == "+")

        def seq_of(n, task):
            if task[-1] == "+":
                return n + 1, task[:-1]
            if task[-1] == "-":
                return n - 1, task[:-1]
            return n, task

        ORDER = {ph: [t for t in MISC_SLOTS.values() if runs(ph, t)] for ph in ("start", "first", "loop", "last")}
        ORDER["tail"] = ["scale3-"]

        def misc_number(phase, n, task):
            before_it = ORDER[phase].index(task)
            if phase == "start":
                return before_it
            if phase == "first":
                return len(ORDER["start"]) + before_it
            whole = len(ORDER["loop"])
            shift = len(ORDER["start"]) + len(ORDER["first"]) - whole
            if phase == "tail":
                return (LAST - 1) * whole + len(ORDER["last"]) + shift + whole + before_it
            return n * whole + (shift + before_it)

        def misc_read(n, task):
            s, name = seq_of(n, task)
            if name[0] in "qk":
                return qk_lo_ready, s * 2 * NP + (2 * int(name[1]) + (name[0] == "k") + 1)
            if name[0] == "v":
                return v_ready, s * NT + (int(name[1]) + 1)
            if name[:5] == "scale":
                return scale_t_ready, s * NP + (int(name[5]) + 1)
            return {"gate_t": gate_t_ready, "xt": xt_lo_ready, "logits": gate_exp_ready}[name], s + 1

        def misc_before(phase, n, task):
            at = ORDER[phase].index(task)
            if at:
                return misc_read(n, ORDER[phase][at - 1])
            if phase == "start":
                return None
            return misc_read(n - 1, ORDER["start" if phase == "first" else "loop"][-1])

        SIDE = {
            "a": ["xt", "qkv0", "qkv1", "qkv2", "qkv3", "wo-", "ot", "fc"],
            "b": ["xt", "qkv0", "qkv1", "qkv2", "qkv3", "wo-", "qt", "ctx0", "ctx1", "ctx2", "att0", "att1",
                  "ot", "fc"],
            None: ["wo-"],
        }
        A_LONE = len(SIDE["a"]) - 1
        A_PERIODS = B - A_AHEAD
        first_side = A_AHEAD * A_LONE
        a_side = first_side + A_LONE
        b_side = a_side + (A_PERIODS - 1) * len(SIDE["a"])
        end_side = b_side + B * len(SIDE["b"])

        def side_number(phase, layer, n, task):
            order = [t for t in SIDE[layer] if t != "wo-" or phase not in ("start", "first")]
            at = order.index(task)
            if phase == "start":
                return n * A_LONE + at
            if phase == "first":
                return first_side + at
            if layer == "a":
                return n * len(order) + (a_side - len(order) + at)
            if layer == "b":
                return n * len(order) + (b_side - B_FROM * len(order) + at)
            return end_side + (n - (B_FROM + B))

        def side_read(layer, n, m, task):
            if task == "wo-":
                return f_x_done, n
            if task[:3] == "qkv":
                return s_qkv_ready, side_seq(layer, m) * NT + (int(task[3]) + 1)
            if task[:3] == "ctx":
                return b_cum_ready, m * (NB - 1) + min(3 * int(task[3]) + 3, NB - 1)
            if task[:3] == "att":
                return s_o_ready, outputs_before("b", m) + (int(task[3]) + 1)
            if task == "qt":
                return b_qt_ready, m + 1
            return {"xt": s_xt_ready, "ot": s_ot_ready}[task], side_seq(layer, m) + 1

        def outputs_before(layer, m):
            return m if layer == "a" else m * 2 + B

        def side_seq(layer, m):
            return m if layer == "a" else m + B

        def by_act(u):
            return u % 8 not in (1, 5)

        def moved_by_act(u):
            return sum(by_act(k) for k in range(u + 1))

        ACT_MOVES = moved_by_act(UNITS - 1)
        DVE_MOVES = UNITS - ACT_MOVES

        def moved(n, u):
            s = n
            if u < 0:
                s, u = n - 1, u + UNITS
            if by_act(u):
                return turned_by_act, s * ACT_MOVES + moved_by_act(u)
            return turned_by_dve, s * DVE_MOVES + (u + 1 - moved_by_act(u))

        LOW, HIGH = slice(0, FD), slice(FD, 2 * FD)

        block = ctx.enter_context(nc.Block())

        def tile_of(ap, t, w=P):
            return ap[:, t * w:(t + 1) * w]

        @block.sync
        def _(sp):
            sp.dma_start(x_all[:, 0, :].rearrange("p (t c) -> p t c", t=NT),
                         x_in[0].rearrange("(t p) c -> p t c", p=P)).then_inc(loaded_x, 16)
            for k, w in enumerate((a_wq, a_wk, a_wv, a_wfc)):
                sp.dma_start(raw_sq[:, k, :], w).then_inc(loaded_w, 16)
            sp.dma_start(raw_sq[:, 4:7, :], b_wqkv.rearrange("(k p) c -> p k c", p=P)).then_inc(loaded_w, 16)
            sp.dma_start(raw_sq[:, 7, :], b_wout).then_inc(loaded_w, 16)
            sp.dma_start(x_all[:, 1:B, :].rearrange("p b (t c) -> p b t c", t=NT),
                         x_in[1:B].rearrange("b (t p) c -> p b t c", p=P)).then_inc(loaded_x, 16)
            sp.dma_start(raw_wq, f_wq).then_inc(loaded_f, 16)
            sp.dma_start(raw_wkv, f_wkv).then_inc(loaded_f, 16)
            sp.dma_start(raw_ws[:, :], f_ws).then_inc(loaded_f, 16)
            sp.dma_start(wo[:, :, :], f_wo.rearrange("(p a) d c -> (a d) p c", a=2)).then_inc(loaded_f, 16)
            sp.dma_start(bo[:, :], f_bo).then_inc(loaded_f, 16)
            with sp.Fori(0, B) as b:
                sp.wait_ge(f_x_done, b + (B + 1))
                sp.dma_start(out[bass.ds(b, 1)].rearrange("b (t p) c -> p (b t) c", p=P),
                             x_all[:, bass.ds(b + B, 1), :].rearrange("p b (t c) -> p (b t) c", t=NT)
                             ).then_inc(stored, 16)
            sp.wait_ge(stored, 16 * B)

        @block.gpsimd
        def _(pool):
            links = [0]

            def link(ins):
                links[0] += 1
                ins.then_inc(p_chain, 1)
                pool.wait_ge(p_chain, links[0])

            link(nc.gpsimd.memset(ident[:, :], 0.0))
            nc.gpsimd.affine_select(out=ident[:, :], in_=ident[:, :], compare_op=ALU.not_equal, fill=1.0,
                                    base=0, pattern=[[-1, P]], channel_multiplier=1).then_inc(ident_done, 1)
            nc.gpsimd.memset(minus_half[:, :], -0.5).then_inc(masks_done, 1)
            link(nc.gpsimd.memset(ctx_mask[:, :], 1.0))
            for view, width in ((ctx_mask[:, 0:C], AD), (ctx_mask[:, C:CW], 1)):
                v = view.rearrange("p (h d) -> p h d", d=width)
                link(nc.gpsimd.affine_select(out=v, in_=v, compare_op=ALU.is_ge, fill=0.0, base=0,
                                             pattern=[[-AD, AH], [0, width]], channel_multiplier=1))
                link(nc.gpsimd.affine_select(out=v, in_=v, compare_op=ALU.is_ge, fill=0.0, base=AD - 1,
                                             pattern=[[AD, AH], [0, width]], channel_multiplier=-1))
            link(nc.gpsimd.memset(before[:, :, :], 1.0))
            link(nc.gpsimd.memset(after[:, :, :], 1.0))
            nc.gpsimd.affine_select(out=before[:, :, :], in_=before[:, :, :], compare_op=ALU.is_gt, fill=0.0,
                                    base=0, pattern=[[1, FH], [-1, FH]], channel_multiplier=0)\
                .then_inc(masks_done, 1)
            nc.gpsimd.affine_select(out=after[:, :, :], in_=after[:, :, :], compare_op=ALU.is_gt, fill=0.0,
                                    base=0, pattern=[[-1, FH], [1, FH]], channel_multiplier=0)\
                .then_inc(masks_done, 1)
            nc.gpsimd.memset(b_ctx[:, 0, :], 0.0).then_inc(masks_done, 1)
            pool.wait_ge(masks_done, 4)

            def f_rstd_step(n):
                pool.wait_ge(f_var_ready, n + 1)
                nc.gpsimd.tensor_tensor(f_rstd[:, :], f_var[:, :], minus_half[:, :], ALU.pow)\
                    .then_inc(f_rstd_ready, 1)

            def side_rstd_step(layer, m):
                pool.wait_ge(s_var_ready, side_seq(layer, m) + 1)
                nc.gpsimd.tensor_tensor(s_rstd[:, :], s_var[:, :], minus_half[:, :], ALU.pow)\
                    .then_inc(s_rstd_ready, 1)

            def scale_step(n, p):
                pool.wait_ge(recip_ready, n * NP + (p + 1))
                pool.wait_ge(gate_ready, n + 1)
                nc.gpsimd.tensor_tensor(
                    scale_w[:, :, :, :],
                    gate[:, :, 2 * p:2 * p + 2].rearrange("p t (a o) -> p t a o", o=1).to_broadcast([P, NT, 2, FD]),
                    recip[:, :, :].rearrange("p a (t o) -> p t a o", o=1).to_broadcast([P, NT, 2, FD]),
                    ALU.mult).then_inc(scale_ready, 1)

            def a_scores_step(m, t):
                pool.wait_ge(s_qkv_ready, m * NT + (t + 1))
                pool.wait_ge(a_prod_used, m * 2 * NT + (t + 1))
                q = s_qkv[:, t, 0:C].rearrange("p (h o d) -> p h o d", h=AH, o=1)
                k = s_qkv[:, t, C:2 * C].rearrange("p (o t d) -> p o t d", o=1, t=AH)
                nc.gpsimd.tensor_tensor(
                    a_prod[:, t % 2, :].rearrange("p (h t d) -> p h t d", h=AH, t=AH),
                    q.to_broadcast([P, AH, AH, AD]), k.to_broadcast([P, AH, AH, AD]),
                    ALU.mult).then_inc(a_prod_ready, 1)

            def a_values_step(m, t):
                if t == 0:
                    pool.wait_ge(a_p_ready, m + 1)
                pool.wait_ge(a_prod_used, m * 2 * NT + (NT + t + 1))
                w = a_p[:, t * AH:(t + 1) * AH, :].rearrange("p h (o t) -> p h o t", o=1)
                v = s_qkv[:, t, 2 * C:3 * C].rearrange("p (o d t) -> p o d t", o=1, t=AH)
                nc.gpsimd.tensor_tensor(
                    a_prod[:, t % 2, :].rearrange("p (h d t) -> p h d t", h=AH, d=AD),
                    w.to_broadcast([P, AH, AD, AH]), v.to_broadcast([P, AH, AD, AH]),
                    ALU.mult).then_inc(a_prod_ready, 1)

            def b_mask_step(m, n):
                pool.wait_ge(b_cum_ready, m * (NB - 1) + n)
                nc.gpsimd.tensor_tensor(b_ctx[:, n, :], b_cum[:, n, :], ctx_mask[:, :], ALU.mult)\
                    .then_inc(b_ctx_ready, 1)

            def period(phase, n, layer, m):
                if phase != "first":
                    scale_step(n - 1, NP - 1)
                if layer == "a":
                    side_rstd_step("a", m)
                    a_scores_step(m, 0)
                    a_scores_step(m, 1)
                    a_scores_step(m, 2)
                    scale_step(n, 0)
                    a_scores_step(m, 3)
                    scale_step(n, 1)
                    f_rstd_step(n + 1)
                    a_values_step(m, 0)
                    a_values_step(m, 1)
                    scale_step(n, 2)
                    a_values_step(m, 2)
                    a_values_step(m, 3)
                    return
                if layer == "b":
                    side_rstd_step("b", m)
                scale_step(n, 0)
                scale_step(n, 1)
                if phase != "last":
                    f_rstd_step(n + 1)
                if layer == "b":
                    for k in range(1, NB):
                        b_mask_step(m, k)
                scale_step(n, 2)

            def tail():
                scale_step(LAST, NP - 1)

            for m in range(A_AHEAD):
                side_rstd_step("a", m)
                for t in range(NT):
                    a_scores_step(m, t)
                for t in range(NT):
                    a_values_step(m, t)
            f_rstd_step(0)
            period("first", 0, "a", A_AHEAD)
            with pool.Fori(1, A_PERIODS) as n:
                period("loop", n, "a", n + A_AHEAD)
            with pool.Fori(0, B) as m:
                period("loop", m + B_FROM, "b", m)
            period("loop", LAST - 1, None, 0)
            period("last", LAST, None, 0)
            tail()

        @block.scalar
        def _(act):
            act.wait_ge(ones_done, 2)
            act.wait_ge(loaded_f, 5 * 16)
            nc.scalar.activation(w_hi[:, 0:FC], raw_wq, ACT.Copy, scale=F_SCALE).then_inc(w_hi_done, 1)
            nc.scalar.activation(w_hi[:, FC:3 * FC], raw_wkv, ACT.Copy).then_inc(w_hi_done, 1)
            nc.scalar.activation(ws_hi[:, :], raw_ws[:, :], ACT.Copy).then_inc(w_hi_done, 1)

            def misc_step(phase, n, task):
                act.wait_ge(misc_full, misc_number(phase, n, task) + 1)
                name = seq_of(n, task)[1]
                if name == "xt":
                    nc.scalar.activation(xt_hi[:, :], misc[:, :], ACT.Copy).then_inc(xt_hi_ready, 1)
                if name == "logits":
                    nc.scalar.activation(g_exp[:, :, :], misc[:, 0:NT * FH].rearrange("p (t h) -> p t h", t=NT),
                                         ACT.Exp, scale=-1.0).then_inc(gate_exp_ready, 1)
                if name == "gate_t":
                    nc.scalar.activation(gate_t[:, :], misc[0:FH, :], ACT.Copy).then_inc(gate_t_ready, 1)
                if name[:5] == "scale":
                    nc.scalar.activation(scale_t[:, :], misc[:, :], ACT.Copy).then_inc(scale_t_ready, 1)
                if name[0] == "v":
                    nc.scalar.activation(v_sb[:, int(name[1]), :], misc[:, :], ACT.Copy).then_inc(v_ready, 1)
                if name[0] == "q":
                    p = int(name[1]) % 2
                    nc.scalar.activation(q_both[LOW, p, 0, :], misc[LOW, :], ACT.Copy)
                    nc.scalar.activation(q_both[HIGH, p, 1, :], misc[HIGH, :], ACT.Copy).then_inc(qk_hi_ready, 1)
                if name[0] == "k":
                    p = int(name[1]) % 2
                    nc.scalar.activation(k_hi[:, p, :], misc[:, :], ACT.Copy)
                    nc.scalar.activation(k_cross[HIGH, p, 0, :], misc[LOW, :], ACT.Copy)
                    nc.scalar.activation(k_cross[LOW, p, 1, :], misc[HIGH, :], ACT.Copy).then_inc(qk_hi_ready, 1)

            def side_filled(phase, layer, n, task):
                act.wait_ge(side_full, side_number(phase, layer, n, task) + 1)

            def exp_step(n, u):
                act.wait_ge(max_ready, n * UNITS + (u + 1))
                nc.scalar.activation(probs[:, u % 4, :], scores[u % 3][:, :], ACT.Exp,
                                     bias=neg_max[:, u:u + 1], accum_out=row_sum[:, u:u + 1]).then_inc(exp_done, 1)

            def move_step(n, u):
                act.wait_ge(turned_ready, n * UNITS + (u + 1))
                h, t = u // NT, u % NT
                nc.scalar.activation(probs_t[:, h % 4, :, t * P:(t + 1) * P],
                                     turned[u % 2][:, :].rearrange("p (c q) -> p c q", c=NT), ACT.Copy)\
                    .then_inc(turned_by_act, 1)

            def side_xt(phase, layer, n, m):
                side_filled(phase, layer, n, "xt")
                nc.scalar.activation(s_xt[:, :], side[:, :], ACT.Copy).then_inc(s_xt_ready, 1)

            def side_qkv(phase, layer, n, m, t):
                side_filled(phase, layer, n, f"qkv{t}")
                nc.scalar.activation(s_qkv[:, t, 0:3 * C], side[:, 0:3 * C], ACT.Copy).then_inc(s_qkv_ready, 1)

            def side_ot(phase, layer, n, m):
                side_filled(phase, layer, n, "ot")
                nc.scalar.activation(s_ot[:, :], side[:, :], ACT.Copy).then_inc(s_ot_ready, 1)

            def a_exp(m):
                act.wait_ge(a_s_ready, m + 1)
                nc.scalar.activation(a_p[:, :, :], a_s[:, :, :], ACT.Exp, scale=A_SCALE).then_inc(a_p_ready, 1)

            def b_exp(m):
                act.wait_ge(b_q_ready, m + 1)
                nc.scalar.activation(b_e[:, :, :], b_q[:, :, :], ACT.Exp).then_inc(b_e_ready, 1)
                for k in range(2):
                    rows = slice(k * BUCKET, (k + 1) * BUCKET)
                    nc.scalar.activation(b_k[rows, k, :, :], s_qkv[rows, :, C:2 * C], ACT.Exp).then_inc(b_k_ready, 1)

            def b_qt_step(phase, n, m):
                side_filled(phase, "b", n, "qt")
                nc.scalar.activation(b_qt[:, :], side[:, :], ACT.Copy).then_inc(b_qt_ready, 1)

            def side_slot(phase, layer, n, m, u):
                if not layer:
                    return
                if u == 3:
                    side_xt(phase, layer, n, m)
                if 5 <= u < 5 + NT:
                    side_qkv(phase, layer, n, m, u - 5)
                if layer == "a":
                    if u == 18:
                        a_exp(m)
                    if u == 31:
                        side_ot(phase, "a", n, m)
                else:
                    if u == 11:
                        b_exp(m)
                    if u == 14:
                        b_qt_step(phase, n, m)
                    if u == 26:
                        side_ot(phase, "b", n, m)

            def period(phase, n, layer, m):
                for u in range(UNITS):
                    if by_act(u):
                        move_step(n, u)
                    if u + 2 < UNITS:
                        exp_step(n, u + 2)
                    elif phase != "last":
                        exp_step(n + 1, u + 2 - UNITS)
                    if u in MISC_SLOTS and runs(phase, MISC_SLOTS[u]):
                        misc_step(phase, n, MISC_SLOTS[u])
                    side_slot(phase, layer, n, m, u)

            def tail():
                misc_step("tail", PERIODS, "scale3-")

            for m in range(A_AHEAD):
                side_xt("start", "a", m, m)
                for t in range(NT):
                    side_qkv("start", "a", m, m, t)
                a_exp(m)
                side_ot("start", "a", m, m)
            for task in ORDER["start"]:
                misc_step("start", -1, task)
            exp_step(0, 0)
            exp_step(0, 1)
            period("first", 0, "a", A_AHEAD)
            with act.Fori(1, A_PERIODS) as n:
                period("loop", n, "a", n + A_AHEAD)
            with act.Fori(0, B) as m:
                period("loop", m + B_FROM, "b", m)
            period("loop", LAST - 1, None, 0)
            period("last", LAST, None, 0)
            tail()

        F_LINKS = 8
        A_LINKS = 4
        B_LINKS = 9
        A_SCORES_SLOTS = [9, 12, 14, 17]
        A_VALUES_SLOTS = [22, 24, 27, 30]

        @block.vector
        def _(dve):
            dve.sem_inc(a_prod_used, 2)
            dve.sem_inc(b_x_done, 1)
            nc.vector.memset(s_qkv[:, :, 3 * C:3 * C + AH], 1.0).then_inc(ones_done, 1)

            nc.vector.memset(b_k[:, :, :, :], 0.0).then_inc(ones_done, 1)

            dve.wait_ge(w_turned, 1)
            nc.vector.tensor_copy(a_w[:, 0:2 * C], scores[0][:, 0:2 * C]).then_inc(w_copied, 1)
            nc.vector.tensor_copy(a_w[:, 2 * C:3 * C].rearrange("p (d t) -> p d t", d=AD),
                                  scores[0][:, 2 * C:3 * C].rearrange("p (t d) -> p d t", d=AD)).then_inc(w_copied, 1)
            nc.vector.tensor_copy(a_fc[:, :], scores[0][:, 3 * C:4 * C]).then_inc(w_copied, 1)
            nc.vector.tensor_copy(b_w[:, :], scores[1][:, 0:3 * C]).then_inc(w_copied, 1)
            nc.vector.tensor_copy(b_out[:, :], scores[1][:, 3 * C:4 * C]).then_inc(w_copied, 1)

            def split_weights():
                dve.wait_ge(w_hi_done, 3)
                nc.vector.scalar_tensor_tensor(out=w_lo[:, 0:FC], in0=raw_wq, scalar=F_SCALE,
                                               in1=w_hi[:, 0:FC].bitcast(fp32), op0=ALU.mult, op1=ALU.subtract)\
                    .then_inc(w_lo_done, 1)
                nc.vector.tensor_tensor(w_lo[:, FC:3 * FC], raw_wkv, w_hi[:, FC:3 * FC].bitcast(fp32),
                                        ALU.subtract).then_inc(w_lo_done, 1)
                nc.vector.tensor_tensor(ws_lo[:, :], raw_ws[:, :], ws_hi[:, :].bitcast(fp32), ALU.subtract)\
                    .then_inc(w_lo_done, 1)

            class Links:

                def __init__(self, sem, base, count):
                    self.sem, self.base, self.count, self.k = sem, base, count, 0

                def link(self, ins):
                    self.k += 1
                    ins.then_inc(self.sem, 1)
                    dve.wait_ge(self.sem, self.base + self.k)

                def end(self):
                    assert self.k == self.count, (self.k, self.count)

            def side_filled(phase, layer, n, task):
                dve.wait_ge(side_full, side_number(phase, layer, n, task) + 1)

            def norm_step(links, slot, stats, mv, var, ready):
                for t in range(NT):
                    last = nc.vector.bn_stats(stats[:, t, :],
                                              x_all[:, bass.ds(slot, 1), t * C:(t + 1) * C].rearrange("p o c -> p (o c)"))
                links.link(last)
                dve.nop(nofuse=True)
                for t in range(NT):
                    last = nc.vector.bn_aggr(mv[:, t, :], stats[:, t, :])
                links.link(last)
                nc.vector.tensor_scalar(var[:, :], mv[:, :, 1], EPS, None, ALU.add).then_inc(ready, 1)

            def xn_step(slot, mv, rstd, xn, ready):
                for t in range(NT):
                    last = nc.vector.tensor_scalar(
                        xn[:, t, :], x_all[:, bass.ds(slot, 1), t * C:(t + 1) * C].rearrange("p o c -> p (o c)"),
                        mv[:, t, 0:1], rstd[:, t:t + 1], ALU.subtract, ALU.mult)
                last.then_inc(ready, 1)

            def f_norm(links, n, first):
                if first:
                    dve.wait_ge(a_x_done, n + 1)
                else:
                    dve.wait_ge(a_x_done, B)
                    dve.wait_ge(b_x_done, n - (B - 2))
                norm_step(links, n, f_stats, f_mv, f_var, f_var_ready)

            def f_xn_step(n):
                dve.wait_ge(f_rstd_ready, n + 1)
                xn_step(n, f_mv, f_rstd, f_xn, f_xn_ready)

            def lower_parts(n, task):
                s, name = seq_of(n, task)
                if name == "xt":
                    dve.wait_ge(xt_hi_ready, s + 1)
                    nc.vector.tensor_tensor(xt_lo[:, :], misc[:, :], xt_hi[:, :].bitcast(fp32), ALU.subtract)\
                        .then_inc(xt_lo_ready, 1)
                    return
                if name[0] not in "qk":
                    return
                p = int(name[1])
                dve.wait_ge(qk_hi_ready, s * 2 * NP + (2 * p + (name[0] == "k") + 1))
                for a, (own, other) in enumerate(((LOW, HIGH), (HIGH, LOW))):
                    if name[0] == "q":
                        last = nc.vector.tensor_tensor(q_both[other, p % 2, a, :], misc[own, :],
                                                       q_both[own, p % 2, a, :].bitcast(fp32), ALU.subtract)
                    else:
                        last = nc.vector.tensor_tensor(k_cross[own, p % 2, a, :], misc[own, :],
                                                       k_hi[own, p % 2, :].bitcast(fp32), ALU.subtract)
                last.then_inc(qk_lo_ready, 1)

            def gate_step(links, n):
                dve.wait_ge(gate_exp_ready, n + 1)
                links.link(nc.vector.tensor_scalar(g_den[:, :, :], g_exp[:, :, :], 1.0, None, ALU.add))
                links.link(nc.vector.reciprocal(g_sig[:, :, :], g_den[:, :, :]))
                mine = g_sig[:, :, :].rearrange("p t (h o) -> p t h o", o=1).to_broadcast([P, NT, FH, FH])
                other = g_sig[:, :, :].rearrange("p t (o h) -> p t o h", o=1).to_broadcast([P, NT, FH, FH])
                nc.vector.tensor_tensor(g_gt[:, :, :, :], other, mine, ALU.is_gt)
                links.link(nc.vector.tensor_tensor(g_ge[:, :, :, :], other, mine, ALU.is_ge))

                def over_tiles(m):
                    return m[:, :, :].rearrange("p h (o k) -> p o h k", o=1).to_broadcast([P, NT, FH, FH])

                nc.vector.tensor_tensor(g_gt[:, :, :, :], g_gt[:, :, :, :], over_tiles(after), ALU.mult)
                links.link(nc.vector.tensor_tensor(g_ge[:, :, :, :], g_ge[:, :, :, :], over_tiles(before), ALU.mult))
                links.link(nc.vector.tensor_tensor(g_ge[:, :, :, :], g_ge[:, :, :, :], g_gt[:, :, :, :], ALU.add))
                links.link(nc.vector.reduce_sum(g_rank[:, :, :], g_ge[:, :, :, :], AX.X))
                nc.vector.scalar_tensor_tensor(out=gate[:, :, :], in0=g_rank[:, :, :], scalar=TOPK - 0.5,
                                               in1=g_sig[:, :, :], op0=ALU.is_lt, op1=ALU.mult)\
                    .then_inc(gate_ready, 1)

            def max_step(n, u):
                dve.wait_ge(scores_ready, n * UNITS + (u + 1))
                nc.vector.tensor_reduce(neg_max[:, u:u + 1], scores[u % 3][:, :], AX.X, ALU.max, negate=True)\
                    .then_inc(max_ready, 1)

            def move_step(n, u):
                dve.wait_ge(turned_ready, n * UNITS + (u + 1))
                h, t = u // NT, u % NT
                nc.vector.tensor_copy(probs_t[:, h % 4, :, t * P:(t + 1) * P],
                                      turned[u % 2][:, :].rearrange("p (c q) -> p c q", c=NT)).then_inc(turned_by_dve, 1)

            def recip_step(n, p):
                dve.wait_ge(exp_done, n * UNITS + PAIR * (p + 1))
                nc.vector.reciprocal(recip[:, :, :], row_sum[:, PAIR * p:PAIR * (p + 1)]
                                     .rearrange("p (a t) -> p a t", a=2)).then_inc(recip_ready, 1)

            def out_step(n, p):
                dve.wait_ge(heads_ready, n * NP + (p + 1))
                dve.wait_ge(scale_t_ready, n * NP + (p + 1))
                nc.vector.tensor_tensor(out_t[:, p, :], heads_out[:, :], scale_t[:, :], ALU.mult)\
                    .then_inc(heads_scaled, 1)

            def add_step(dst, src, bank_ap, done):
                nc.vector.tensor_tensor(x_all[:, bass.ds(dst, 1), :].rearrange("p o c -> p (o c)"), bank_ap,
                                        x_all[:, bass.ds(src, 1), :].rearrange("p o c -> p (o c)"), ALU.add)\
                    .then_inc(done, 1)

            def wo_step(phase, layer, n):
                side_filled(phase, layer, n, "wo-")
                add_step(n - 1, n - 1, side[:, :], f_x_done)

            def a_norm(links, m, wait_load):
                if wait_load:
                    dve.wait_ge(loaded_x, 16 if m == 0 else 32)
                norm_step(links, m, s_stats, s_mv, s_var, s_var_ready)

            def side_xn(layer, m):
                dve.wait_ge(s_rstd_ready, side_seq(layer, m) + 1)
                xn_step(m, s_mv, s_rstd, s_xn, s_xn_ready)

            def a_scores_sum(m, t):
                dve.wait_ge(a_prod_ready, m * 2 * NT + (t + 1))
                nc.vector.reduce_sum(a_s[:, t * AH:(t + 1) * AH, :],
                                            a_prod[:, t % 2, :].rearrange("p (h t d) -> p h t d", h=AH, t=AH),
                                            AX.X).then_inc(a_prod_used, 1)

            def a_softmax(links, m):
                dve.wait_ge(a_prod_used, m * 2 * NT + (NT + 2))
                links.link(nc.vector.reduce_max(a_max[:, :], a_s[:, :, :], AX.X))
                nc.vector.tensor_tensor(a_s[:, :, :], a_s[:, :, :],
                                        a_max[:, :].rearrange("p (h o) -> p h o", o=1)
                                        .to_broadcast([P, NT * AH, AH]), ALU.subtract).then_inc(a_s_ready, 1)

            def a_sums(links, m):
                dve.wait_ge(a_p_ready, m + 1)
                links.link(nc.vector.reduce_sum(a_sum[:, :], a_p[:, :, :], AX.X))
                nc.vector.reciprocal(a_rec[:, :], a_sum[:, :])

            def a_values_sum(m, t):
                dve.wait_ge(a_prod_ready, m * 2 * NT + (NT + t + 1))
                nc.vector.reduce_sum(s_o[:, t, :].rearrange("p (h d) -> p h d", h=AH),
                                            a_prod[:, t % 2, :].rearrange("p (h d t) -> p h d t", h=AH, d=AD),
                                            AX.X).then_inc(a_prod_used, 1)

            def a_normalise(m):
                dve.wait_ge(a_prod_used, m * 2 * NT + (2 * NT + 2))
                o = s_o[:, :, :].rearrange("p t (h d) -> p (t h) d", d=AD)
                nc.vector.tensor_tensor(o, o, a_rec[:, :].rearrange("p (h o) -> p h o", o=1)
                                        .to_broadcast([P, NT * AH, AD]), ALU.mult).then_inc(s_o_ready, 1)

            def side_add(phase, layer, n, m):
                side_filled(phase, layer, n, "fc")
                if layer == "a":
                    add_step(m, m, side[:, :], a_x_done)
                else:
                    add_step(m + B, m, side[:, :], b_x_done)

            def b_norm(links, m):
                dve.wait_ge(f_x_done, m + 1)
                norm_step(links, m, s_stats, s_mv, s_var, s_var_ready)

            def b_query_max(links, m):
                dve.wait_ge(s_qkv_ready, (m + (B + 1)) * NT)
                q = s_qkv[:, :, 0:C].rearrange("p t (h d) -> p t h d", d=AD)
                top = a_max[:, :].rearrange("p (t h) -> p t h", t=NT)
                links.link(nc.vector.reduce_max(top, q, AX.X))
                nc.vector.tensor_tensor(b_q[:, :, :].rearrange("p t (h d) -> p t h d", d=AD), q,
                                        top.rearrange("p t (h o) -> p t h o", o=1).to_broadcast([P, NT, AH, AD]),
                                        ALU.subtract).then_inc(b_q_ready, 1)

            def b_query_softmax(links, m):
                dve.wait_ge(b_e_ready, m + 1)
                e = b_e[:, :, :].rearrange("p t (h d) -> p (t h) d", d=AD)
                links.link(nc.vector.reduce_sum(a_sum[:, :], e, AX.X))
                links.link(nc.vector.reciprocal(a_rec[:, :], a_sum[:, :]))
                nc.vector.scalar_tensor_tensor(
                    out=b_q[:, :, :].rearrange("p t (h d) -> p (t h) d", d=AD), in0=e, scalar=A_SCALE,
                    in1=a_rec[:, :].rearrange("p (h o) -> p h o", o=1).to_broadcast([P, NT * AH, AD]),
                    op0=ALU.mult, op1=ALU.mult).then_inc(b_qn_ready, 1)

            def b_sums(phase, n, m, g):
                side_filled(phase, "b", n, f"ctx{g}")
                for k in range(3 * g, min(3 * g + 3, NB - 1)):
                    j = (k - 3 * g) * CW
                    if k == 0:
                        ins = nc.vector.tensor_copy(b_cum[:, 1, :], side[:, 0:CW])
                    else:
                        dve.wait_ge(b_cum_ready, m * (NB - 1) + k)
                        ins = nc.vector.tensor_tensor(b_cum[:, k + 1, :], side[:, j:j + CW], b_cum[:, k, :], ALU.add)
                    ins.then_inc(b_cum_ready, 1)

            def b_attend(phase, links, n, m, g):
                side_filled(phase, "b", n, f"att{g}")
                a = side[:, 0:2 * CW].rearrange("p (t c) -> p t c", t=2)
                links.link(nc.vector.tensor_scalar(b_den[:, :, :], a[:, :, C:CW], 1e-6, None, ALU.max))
                links.link(nc.vector.reciprocal(b_inv[:, :, :], b_den[:, :, :]))
                nc.vector.tensor_tensor(
                    s_o[:, 2 * g:2 * g + 2, :].rearrange("p t (h d) -> p t h d", d=AD),
                    a[:, :, 0:C].rearrange("p t (h d) -> p t h d", d=AD),
                    b_inv[:, :, :].rearrange("p t (h o) -> p t h o", o=1).to_broadcast([P, 2, AH, AD]),
                    ALU.mult).then_inc(s_o_ready, 1)

            def side_slot(phase, layer, links, n, m, u):
                if layer == "a":
                    if u == 0:
                        a_norm(links, m, False)
                    if u == 1:
                        side_xn("a", m)
                    if u in A_SCORES_SLOTS:
                        a_scores_sum(m, A_SCORES_SLOTS.index(u))
                        if u == A_SCORES_SLOTS[-1]:
                            a_softmax(links, m)
                    if u == A_SCORES_SLOTS[-1] + 2:
                        a_sums(links, m)
                    if u in A_VALUES_SLOTS:
                        a_values_sum(m, A_VALUES_SLOTS.index(u))
                        if u == A_VALUES_SLOTS[-1]:
                            a_normalise(m)
                if layer == "b":
                    if u == 0:
                        b_norm(links, m)
                    if u == 1:
                        side_xn("b", m)
                    if u == 10:
                        b_query_max(links, m)
                    if u == 12:
                        b_query_softmax(links, m)
                    if u in (16, 18, 20):
                        b_sums(phase, n, m, (u - 16) // 2)
                    if u in (23, 25):
                        b_attend(phase, links, n, m, (u - 23) // 2)
                    if u == 29:
                        side_add(phase, "b", n, m)

            def period(phase, n, layer, m):
                links = Links(f_chain, n * F_LINKS + 2, F_LINKS if phase != "last" else F_LINKS - 2)
                side_links = Links(s_chain, m * A_LINKS, A_LINKS) if layer == "a" else \
                    Links(s_chain, m * B_LINKS + B * A_LINKS, B_LINKS)
                for u in range(UNITS):
                    if u + 2 < UNITS:
                        max_step(n, u + 2)
                    elif phase != "last":
                        max_step(n + 1, u + 2 - UNITS)
                    if not by_act(u):
                        move_step(n, u)
                    if u in RECIP_SLOTS and runs(phase, RECIP_SLOTS[u]):
                        s, p = seq_of(n, RECIP_SLOTS[u])
                        recip_step(s, int(p))
                    if u - 1 in MISC_SLOTS and runs(phase, MISC_SLOTS[u - 1]):
                        lower_parts(n, MISC_SLOTS[u - 1])
                    if u - 1 in MISC_SLOTS and MISC_SLOTS[u - 1] == "logits":
                        gate_step(links, n)
                    if u in OUT_SLOTS and runs(phase, OUT_SLOTS[u]):
                        s, p = seq_of(n, OUT_SLOTS[u])
                        out_step(s, int(p))
                    if u - NT in WO_SLOTS and WO_SLOTS[u - NT] == 0 and phase != "first":
                        wo_step(phase, layer, n)
                    if phase != "last":
                        if u == NORM_SLOT:
                            f_norm(links, n + 1, None if layer == "b" else n + 1 < B)
                        if u == XN_SLOT:
                            f_xn_step(n + 1)
                    side_slot(phase, layer, side_links, n, m, u)
                links.end()
                if layer == "a":
                    side_add(phase, "a", n, m)
                if layer:
                    side_links.end()

            def tail():
                recip_step(LAST, NP - 1)
                out_step(LAST, NP - 1)
                wo_step("tail", None, PERIODS)

            for m in range(A_AHEAD):
                links = Links(s_chain, m * A_LINKS, A_LINKS)
                a_norm(links, m, True)
                side_xn("a", m)
                if m == 0:
                    split_weights()
                for t in range(NT):
                    a_scores_sum(m, t)
                a_softmax(links, m)
                a_sums(links, m)
                for t in range(NT):
                    a_values_sum(m, t)
                a_normalise(m)
                side_add("start", "a", m, m)
                links.end()
            links = Links(f_chain, 0, 2)
            dve.wait_ge(masks_done, 4)
            f_norm(links, 0, True)
            f_xn_step(0)
            for task in ORDER["start"]:
                lower_parts(-1, task)
            links.end()
            max_step(0, 0)
            max_step(0, 1)
            period("first", 0, "a", A_AHEAD)
            with dve.Fori(1, A_PERIODS) as n:
                period("loop", n, "a", n + A_AHEAD)
            with dve.Fori(0, B) as m:
                period("loop", m + B_FROM, "b", m)
            period("loop", LAST - 1, None, 0)
            period("last", LAST, None, 0)
            tail()

        @block.tensor
        def _(pe):
            pe.wait_ge(ident_done, 1)
            pe.wait_ge(loaded_w, 6 * 16)
            for k in range(8):
                last = nc.tensor.transpose(tile_of(scores[k // 4], k % 4), raw_sq[:, k, :], ident[:, :])
            last.then_inc(w_turned, 1)
            pe.wait_ge(w_copied, 5)

            def misc_claim(phase, n, task):
                event = misc_before(phase, n, task)
                if event:
                    pe.wait_ge(*event)

            def side_claim(phase, layer, n, m, task):
                order = [t for t in SIDE[layer] if t != "wo-" or phase not in ("start", "first")]
                at = order.index(task)
                if at:
                    pe.wait_ge(*side_read(layer, n, m, order[at - 1]))
                elif task == "wo-":
                    pe.wait_ge(b_x_done, B + 1)
                    pe.wait_ge(f_x_done, n - 1)

            def split_product(dst, l_hi, l_lo, r_hi, r_lo):
                nc.tensor.matmul(dst, l_hi, r_lo, start=True, stop=False)
                nc.tensor.matmul(dst, l_lo, r_hi, start=False, stop=False)
                return nc.tensor.matmul(dst, l_hi, r_hi, start=False, stop=True)

            def misc_step(phase, n, task):
                misc_claim(phase, n, task)
                s, name = seq_of(n, task)
                if name == "xt":
                    pe.wait_ge(f_xn_ready, s + 1)
                    for t in range(NT):
                        last = nc.tensor.transpose(tile_of(misc, t), f_xn[:, t, :], ident[:, :])
                if name == "logits":
                    for t in range(NT):
                        last = split_product(misc[:, t * FH:(t + 1) * FH], tile_of(xt_hi, t), tile_of(xt_lo, t),
                                             ws_hi[:, :], ws_lo[:, :])
                if name == "gate_t":
                    pe.wait_ge(gate_ready, s + 1)
                    for t in range(NT):
                        last = nc.tensor.transpose(misc[0:FH, t * P:(t + 1) * P], gate[:, t, :], ident[:, :])
                if name[:5] == "scale":
                    pe.wait_ge(scale_ready, s * NP + (int(name[5]) + 1))
                    for t in range(NT):
                        last = nc.tensor.transpose(tile_of(misc, t),
                                                   scale_w[:, t, :, :].rearrange("p a d -> p (a d)"), ident[:, :])
                if name[0] == "v":
                    t = int(name[1])
                    last = split_product(misc[:, :], tile_of(xt_hi, t), tile_of(xt_lo, t),
                                         w_hi[:, 2 * FC:3 * FC], w_lo[:, 2 * FC:3 * FC])
                if name[0] in "qk":
                    if name == "q0":
                        pe.wait_ge(xt_lo_ready, s + 1)
                    c = (FC if name[0] == "k" else 0) + int(name[1]) * P
                    last = split_product(misc[:, :], w_hi[:, c:c + P], w_lo[:, c:c + P], xt_hi[:, :], xt_lo[:, :])
                last.then_inc(misc_full, 1)

            def scores_step(n, u):
                h, t = u // NT, u % NT
                p, r = h // 2, (h % 2) * FD
                if u % PAIR == 0:
                    pe.wait_ge(qk_lo_ready, n * 2 * NP + (2 * p + 2))
                if u >= 3:
                    pe.wait_ge(exp_done, n * UNITS + (u - 2))
                q = slice(t * P, (t + 1) * P)
                dst = scores[u % 3][:, :]
                nc.tensor.matmul(dst, q_both[:, p % 2, h % 2, q], k_cross[:, p % 2, h % 2, :], start=True, stop=False)
                nc.tensor.matmul(dst, q_both[r:r + FD, p % 2, h % 2, q], k_hi[r:r + FD, p % 2, :],
                                 start=False, stop=True).then_inc(scores_ready, 1)

            def turn_step(phase, n, u):
                pe.wait_ge(exp_done, n * UNITS + (u + 1))
                if u >= 2 or phase != "first":
                    pe.wait_ge(*moved(n, u - 2))
                for c in range(NT):
                    last = nc.tensor.transpose(tile_of(turned[u % 2], c), probs[:, u % 4, c * P:(c + 1) * P],
                                               ident[:, :])
                last.then_inc(turned_ready, 1)

            def pv_step(phase, n, pair, c):
                s, p = seq_of(n, pair)
                p = int(p)
                if c == 0:
                    u = PAIR * (p + 1) - 1
                    pe.wait_ge(turned_by_act, s * ACT_MOVES + moved_by_act(u))
                    pe.wait_ge(turned_by_dve, s * DVE_MOVES + (u + 1 - moved_by_act(u)))
                    if p or phase != "first":
                        pe.wait_ge(heads_scaled, s * NP + p)
                if p == 0:
                    pe.wait_ge(v_ready, s * NT + (c + 1))
                for a in range(2):
                    h = 2 * p + a
                    last = nc.tensor.matmul(heads_out[a * FD:(a + 1) * FD, :], v_sb[:, c, h * FD:(h + 1) * FD],
                                            probs_t[:, h % 4, c, :], start=(c == 0), stop=(c == NT - 1))
                if c == NT - 1:
                    last.then_inc(heads_ready, 1)

            def wo_step(phase, layer, n, m, t):
                if t == 0:
                    side_claim(phase, layer, n, m, "wo-")
                    pe.wait_ge(gate_t_ready, n)
                    pe.wait_ge(heads_scaled, n * NP)
                nc.tensor.matmul(tile_of(side, t), gate_t[:, t * P:(t + 1) * P], bo[:, :], start=True, stop=False)
                for p in range(NP):
                    last = nc.tensor.matmul(tile_of(side, t), out_t[:, p, t * P:(t + 1) * P], wo[:, p, :],
                                            start=False, stop=(p == NP - 1))
                if t == NT - 1:
                    last.then_inc(side_full, 1)

            def side_turn(phase, layer, n, m, task, ready, value, src):
                side_claim(phase, layer, n, m, task)
                pe.wait_ge(ready, value)
                for t in range(NT):
                    last = nc.tensor.transpose(tile_of(side, t), src[:, t, :], ident[:, :])
                last.then_inc(side_full, 1)

            def side_xt(phase, layer, n, m):
                side_turn(phase, layer, n, m, "xt", s_xn_ready, side_seq(layer, m) + 1, s_xn)

            def side_qkv(phase, layer, n, m, t):
                side_claim(phase, layer, n, m, f"qkv{t}")
                if t == 0:
                    pe.wait_ge(s_xt_ready, side_seq(layer, m) + 1)
                w = a_w if layer == "a" else b_w
                nc.tensor.matmul(side[:, 0:3 * C], tile_of(s_xt, t), w[:, :], start=True, stop=True)\
                    .then_inc(side_full, 1)

            def side_ot(phase, layer, n, m):
                side_turn(phase, layer, n, m, "ot", s_o_ready, outputs_before(layer, m) + (1 if layer == "a" else 2), s_o)

            def side_fc(phase, layer, n, m):
                side_claim(phase, layer, n, m, "fc")
                pe.wait_ge(s_ot_ready, side_seq(layer, m) + 1)
                w = a_fc if layer == "a" else b_out
                for t in range(NT):
                    last = nc.tensor.matmul(tile_of(side, t), tile_of(s_ot, t), w[:, :], start=True, stop=True)
                last.then_inc(side_full, 1)

            def b_context(phase, n, m, g):
                side_claim(phase, "b", n, m, f"ctx{g}")
                if g == 0:
                    pe.wait_ge(b_k_ready, m * 2 + 2)
                for k in range(3 * g, min(3 * g + 3, NB - 1)):
                    j, t = (k - 3 * g) * CW, k // 2
                    last = nc.tensor.matmul(side[:, j:j + CW], b_k[:, k % 2, t, :],
                                            s_qkv[:, t, 2 * C:2 * C + CW], start=True, stop=True)
                last.then_inc(side_full, 1)

            def b_attend(phase, n, m, g):
                side_claim(phase, "b", n, m, f"att{g}")
                if g == 0:
                    pe.wait_ge(b_qt_ready, m + 1)
                pe.wait_ge(b_ctx_ready, m * (NB - 1) + (3 if g == 0 else NB - 1))
                for k in range(4 * g, 4 * g + 4):
                    r, j = (k % 2) * BUCKET, (k // 2 - 2 * g) * CW
                    last = nc.tensor.matmul(side[r:r + BUCKET, j:j + CW], b_qt[:, k * BUCKET:(k + 1) * BUCKET],
                                            b_ctx[:, k, :], start=True, stop=True)
                last.then_inc(side_full, 1)

            def side_slot(phase, layer, n, m, u):
                if not layer:
                    return
                if u == 3:
                    side_xt(phase, layer, n, m)
                if 5 <= u < 5 + NT:
                    side_qkv(phase, layer, n, m, u - 5)
                if layer == "b":
                    if u == 14:
                        side_turn(phase, "b", n, m, "qt", b_qn_ready, m + 1, b_q)
                    if u in (15, 17, 19):
                        b_context(phase, n, m, (u - 15) // 2)
                    if u in (22, 24):
                        b_attend(phase, n, m, (u - 22) // 2)
                    if u == 26:
                        side_ot(phase, "b", n, m)
                    if u == 28:
                        side_fc(phase, "b", n, m)

            def period(phase, n, layer, m):
                for u in range(UNITS):
                    if u + 2 < UNITS:
                        scores_step(n, u + 2)
                    turn_step(phase, n, u)
                    if u + 2 >= UNITS and phase != "last":
                        scores_step(n + 1, u + 2 - UNITS)
                    if u in WO_SLOTS and phase != "first":
                        wo_step(phase, layer, n, m, WO_SLOTS[u])
                    if u in PV_SLOTS and runs(phase, PV_SLOTS[u][0]):
                        pv_step(phase, n, *PV_SLOTS[u])
                    if u in MISC_SLOTS and runs(phase, MISC_SLOTS[u]):
                        misc_step(phase, n, MISC_SLOTS[u])
                    side_slot(phase, layer, n, m, u)
                if layer == "a":
                    side_ot(phase, "a", n, m)
                    side_fc(phase, "a", n, m)

            def tail():
                for c in range(NT):
                    pv_step("tail", PERIODS, "3-", c)
                misc_step("tail", PERIODS, "scale3-")
                for t in range(NT):
                    wo_step("tail", None, PERIODS, 0, t)

            for m in range(A_AHEAD):
                side_xt("start", "a", m, m)
                for t in range(NT):
                    side_qkv("start", "a", m, m, t)
                side_ot("start", "a", m, m)
                side_fc("start", "a", m, m)
            pe.wait_ge(w_lo_done, 3)
            for task in ORDER["start"]:
                misc_step("start", -1, task)
            scores_step(0, 0)
            scores_step(0, 1)
            period("first", 0, "a", A_AHEAD)
            with pe.Fori(1, A_PERIODS) as n:
                period("loop", n, "a", n + A_AHEAD)
            with pe.Fori(0, B) as m:
                period("loop", m + B_FROM, "b", m)
            period("loop", LAST - 1, None, 0)
            period("last", LAST, None, 0)
            tail()


_INS = ['L0_attn_a_x', 'L0_attn_a_Wq', 'L0_attn_a_Wk', 'L0_attn_a_Wv', 'L0_attn_a_Wfc', 'L0_attn_b_W_qkv',
        'L0_attn_b_W_out', 'L0_ffn_Wq', 'L0_ffn_Wkv', 'L0_ffn_Ws', 'L0_ffn_Wo', 'L0_ffn_bo']
_OUTS = [((8, 512, 128), 'float32')]


def kernel(**inputs):
    import numpy as _np
    import concourse.bacc as _bacc
    from concourse import mybir as _mybir
    from concourse.bass_utils import run_bass_kernel_spmd as _run

    nc = _bacc.Bacc("TRN2", target_bir_lowering=False, num_devices=1)
    arrays, args = {}, []
    for name in _INS:
        a = _np.ascontiguousarray(inputs[name])
        arrays[f"in_{name}_dram"] = a
        args.append(nc.dram_tensor(f"in_{name}_dram", a.shape, _mybir.dt.from_np(a.dtype), kind="ExternalInput").ap())
    for i, (shape, dtype) in enumerate(_OUTS):
        dt = _mybir.dt.from_np(_np.dtype(dtype))
        args.append(nc.dram_tensor(f"out_{i}_dram", shape, dt, kind="ExternalOutput").ap())
    bass_hybrid_attention_ffn_kernel(nc, *args)
    r = _run(nc, [arrays], core_ids=[0])
    got = tuple(r.results[0][f"out_{i}_dram"] for i in range(len(_OUTS)))
    return got[0]
```

```python
import concourse.bass as bass
from concourse import mybir
from contextlib import ExitStack


def bass_hybrid_attention_ffn_kernel(
    nc: bass.Bass,
    x_in: bass.AP,
    a_wq: bass.AP,
    a_wk: bass.AP,
    a_wv: bass.AP,
    a_wfc: bass.AP,
    b_wqkv: bass.AP,
    b_wout: bass.AP,
    f_wq: bass.AP,
    f_wkv: bass.AP,
    f_ws: bass.AP,
    f_wo: bass.AP,
    f_bo: bass.AP,
    out: bass.AP,
):
    fp32 = mybir.dt.float32
    fp32r = mybir.dt.float32r
    ALU = mybir.AluOpType
    ACT = mybir.ActivationFunctionType
    AX = mybir.AxisListType

    B, T, C = x_in.shape
    P = 128
    NT = T // P
    AH = 16
    AD = C // AH
    FH = f_bo.shape[0]
    FD = f_wo.shape[1]
    FC = FH * FD
    NP = FH // 2
    TOPK = 3
    EPS = 1e-5
    BUCKET = 64
    NB = T // BUCKET
    CW = C + AH
    UNITS = FH * NT
    A_SCALE = float(AD) ** -0.5
    F_SCALE = float(FD) ** -0.5
    PERIODS = 2 * B
    A_AHEAD = 2
    B_FROM = B - A_AHEAD

    ctx = ExitStack()
    with ctx:
        def sb(name, shape, dt=fp32):
            return ctx.enter_context(nc.sbuf_tensor(name, shape, dt))

        def sem(name):
            return ctx.enter_context(nc.semaphore(name))

        x_all = sb("x_all", [P, 2 * B, NT * C])
        ident = sb("ident", [P, P])
        ctx_mask = sb("ctx_mask", [P, CW])
        before = sb("before", [P, FH, FH])
        after = sb("after", [P, FH, FH])
        minus_half = sb("minus_half", [P, NT])
        a_w = sb("a_w", [P, 3 * C])
        a_fc = sb("a_fc", [P, C])
        b_w = sb("b_w", [P, 3 * C])
        b_out = sb("b_out", [P, C])
        raw_ws = sb("raw_ws", [P, FH])
        w_hi = sb("w_hi", [P, 3 * FC], fp32r)
        w_lo = sb("w_lo", [P, 3 * FC], fp32r)
        ws_hi = sb("ws_hi", [P, FH], fp32r)
        ws_lo = sb("ws_lo", [P, FH], fp32r)
        wo = sb("wo", [P, NP, C])
        bo = sb("bo", [FH, C])

        f_stats = sb("f_stats", [P, NT, 6])
        f_mv = sb("f_mv", [P, NT, 2])
        f_var = sb("f_var", [P, NT])
        f_rstd = sb("f_rstd", [P, NT])
        f_xn = sb("f_xn", [P, NT, C])
        xt_hi = sb("xt_hi", [P, T], fp32r)
        xt_lo = sb("xt_lo", [P, T], fp32r)
        q_both = sb("q_both", [P, 2, 2, T], fp32r)
        k_hi = sb("k_hi", [P, 2, T], fp32r)
        k_cross = sb("k_cross", [P, 2, 2, T], fp32r)
        v_sb = sb("v_sb", [P, NT, FC])
        neg_max = sb("neg_max", [P, UNITS])
        row_sum = sb("row_sum", [P, UNITS])
        probs = sb("probs", [P, 4, T])
        probs_t = sb("probs_t", [P, 4, NT, T])
        recip = sb("recip", [P, 2, NT])
        scale_w = sb("scale_w", [P, NT, 2, FD])
        scale_t = sb("scale_t", [P, T])
        out_t = sb("out_t", [P, NP, T])
        raw_wq = probs_t[:, 0, 0, :]
        raw_wkv = probs_t[:, 0, 1:3, :].rearrange("p a c -> p (a c)")
        raw_sq = out_t[:, 0:2, :].rearrange("p a (k c) -> p (a k) c", c=C)
        g_exp = sb("g_exp", [P, NT, FH])
        g_den = sb("g_den", [P, NT, FH])
        g_sig = sb("g_sig", [P, NT, FH])
        g_gt = sb("g_gt", [P, NT, FH, FH])
        g_ge = sb("g_ge", [P, NT, FH, FH])
        g_rank = sb("g_rank", [P, NT, FH])
        gate = sb("gate", [P, NT, FH])
        gate_t = sb("gate_t", [FH, T])

        s_stats = sb("s_stats", [P, NT, 6])
        s_mv = sb("s_mv", [P, NT, 2])
        s_var = sb("s_var", [P, NT])
        s_rstd = sb("s_rstd", [P, NT])
        s_xn = sb("s_xn", [P, NT, C])
        s_xt = sb("s_xt", [P, T])
        s_qkv = sb("s_qkv", [P, NT, 3 * C + AH])
        s_ot = sb("s_ot", [P, T])
        s_o = sb("s_o", [P, NT, C])
        a_prod = sb("a_prod", [P, 2, AH * AH * AD])
        a_own = sb("a_own", [P, AH * AH * AD])
        a_s = sb("a_s", [P, NT * AH, AH])
        a_p = sb("a_p", [P, NT * AH, AH])
        a_max = sb("a_max", [P, NT * AH])
        a_sum = sb("a_sum", [P, NT * AH])
        a_rec = sb("a_rec", [P, NT * AH])
        b_q = sb("b_q", [P, NT, C])
        b_e = sb("b_e", [P, NT, C])
        b_k = sb("b_k", [P, 2, NT, C])
        b_cum = a_prod[:, :, :].rearrange("p a n -> p (a n)")[:, 0:NB * CW].rearrange("p (n c) -> p n c", c=CW)
        b_ctx = sb("b_ctx", [P, NB, CW])
        b_qt = sb("b_qt", [P, T])
        b_den = sb("b_den", [P, 2, AH])
        b_inv = sb("b_inv", [P, 2, AH])

        def bank(name):
            return ctx.enter_context(nc.psum_tensor(name, [P, 512], fp32))

        scores = [bank(f"scores{i}") for i in range(3)]
        turned = [bank(f"turned{i}") for i in range(2)]
        heads_out = bank("heads_out")
        misc = bank("misc")
        side = bank("side")

        loaded_x = sem("loaded_x")
        loaded_w = sem("loaded_w")
        loaded_f = sem("loaded_f")
        ident_done = sem("ident_done")
        masks_done = sem("masks_done")
        ones_done = sem("ones_done")
        w_turned = sem("w_turned")
        w_copied = sem("w_copied")
        w_hi_done = sem("w_hi_done")
        w_lo_done = sem("w_lo_done")
        f_chain = sem("f_chain")
        s_chain = sem("s_chain")
        p_chain = sem("p_chain")
        f_var_ready = sem("f_var_ready")
        f_rstd_ready = sem("f_rstd_ready")
        f_xn_ready = sem("f_xn_ready")
        xt_hi_ready = sem("xt_hi_ready")
        xt_lo_ready = sem("xt_lo_ready")
        qk_hi_ready = sem("qk_hi_ready")
        qk_lo_ready = sem("qk_lo_ready")
        v_ready = sem("v_ready")
        misc_full = sem("misc_full")
        scores_ready = sem("scores_ready")
        max_ready = sem("max_ready")
        exp_done = sem("exp_done")
        turned_ready = sem("turned_ready")
        moved = sem("moved")
        heads_ready = sem("heads_ready")
        heads_scaled = sem("heads_scaled")
        recip_ready = sem("recip_ready")
        scale_ready = sem("scale_ready")
        scale_t_ready = sem("scale_t_ready")
        gate_exp_ready = sem("gate_exp_ready")
        gate_ready = sem("gate_ready")
        gate_t_ready = sem("gate_t_ready")
        f_x_done = sem("f_x_done")
        side_full = sem("side_full")
        s_var_ready = sem("s_var_ready")
        s_rstd_ready = sem("s_rstd_ready")
        s_xn_ready = sem("s_xn_ready")
        s_xt_ready = sem("s_xt_ready")
        s_qkv_ready = sem("s_qkv_ready")
        s_o_ready = sem("s_o_ready")
        s_ot_ready = sem("s_ot_ready")
        a_prod_ready = sem("a_prod_ready")
        a_prod_used = sem("a_prod_used")
        a_own_summed = sem("a_own_summed")
        a_s_ready = sem("a_s_ready")
        a_p_ready = sem("a_p_ready")
        a_x_done = sem("a_x_done")
        b_q_ready = sem("b_q_ready")
        b_e_ready = sem("b_e_ready")
        b_k_ready = sem("b_k_ready")
        b_qn_ready = sem("b_qn_ready")
        b_qt_ready = sem("b_qt_ready")
        b_cum_ready = sem("b_cum_ready")
        b_ctx_ready = sem("b_ctx_ready")
        b_x_done = sem("b_x_done")
        stored = sem("stored")

        PAIR = 2 * NT
        LAST = PERIODS - 1
        MISC_SLOTS = {0: "q1", 2: "k1", 4: "scale3-", 5: "logits", 6: "v0", 7: "v1", 8: "q2", 10: "v2", 11: "v3",
                      12: "k2", 14: "scale0", 15: "gate_t", 16: "q3", 18: "k3", 20: "scale1", 22: "xt+",
                      24: "q0+", 26: "k0+", 28: "scale2"}
        PV_SLOTS = {PAIR * p + 1 + c: (f"{p - 1}" if p else f"{NP - 1}-", c) for p in range(NP) for c in range(NT)}
        RECIP_SLOTS = {PAIR * p: (f"{p - 1}" if p else f"{NP - 1}-") for p in range(NP)}
        OUT_SLOTS = {5: f"{NP - 1}-", 15: "0", 21: "1", 29: "2"}
        WO_SLOTS = {9 + t: t for t in range(NT)}
        NORM_SLOT, XN_SLOT = 10, 14
        SIDE_NORM, SIDE_XN, SIDE_XT, SIDE_QKV = 1, 3, 4, 5
        A_SCORES_SLOTS = [8, 11, 13, 10]
        A_VALUES_SLOTS = [18, 21, 24, 20]
        A_SOFTMAX, A_EXP, A_SUMS, A_NORMALISE, A_OT, A_FC = 14, 15, 16, 25, 27, 29
        B_MAX, B_EXP, B_SOFTMAX, B_QT = 10, 12, 13, 15
        B_CTX, B_ATT, B_OT, B_FC = (16, 18, 20), (23, 25), 27, 29

        def runs(phase, task):
            if phase == "start":
                return task[-1] == "+"
            return not (phase == "first" and task[-1] == "-" or phase == "last" and task[-1] == "+")

        def seq_of(n, task):
            if task[-1] == "+":
                return n + 1, task[:-1]
            if task[-1] == "-":
                return n - 1, task[:-1]
            return n, task

        ORDER = {ph: [t for t in MISC_SLOTS.values() if runs(ph, t)] for ph in ("start", "first", "loop", "last")}
        ORDER["tail"] = ["scale3-"]

        def misc_number(phase, n, task):
            before_it = ORDER[phase].index(task)
            if phase == "start":
                return before_it
            if phase == "first":
                return len(ORDER["start"]) + before_it
            whole = len(ORDER["loop"])
            shift = len(ORDER["start"]) + len(ORDER["first"]) - whole
            if phase == "tail":
                return (LAST - 1) * whole + len(ORDER["last"]) + shift + whole + before_it
            return n * whole + (shift + before_it)

        def misc_read(n, task):
            s, name = seq_of(n, task)
            if name[0] in "qk":
                return qk_lo_ready, s * 2 * NP + (2 * int(name[1]) + (name[0] == "k") + 1)
            if name[0] == "v":
                return v_ready, s * NT + (int(name[1]) + 1)
            if name[:5] == "scale":
                return scale_t_ready, s * NP + (int(name[5]) + 1)
            return {"gate_t": gate_t_ready, "xt": xt_lo_ready, "logits": gate_exp_ready}[name], s + 1

        def misc_before(phase, n, task):
            at = ORDER[phase].index(task)
            if at:
                return misc_read(n, ORDER[phase][at - 1])
            if phase == "start":
                return None
            return misc_read(n - 1, ORDER["start" if phase == "first" else "loop"][-1])

        def pool_tiles(phase):
            return NT // 2 if phase == "start" else NT - 1

        def pool_products(phase, m):
            if phase == "start":
                return m * NT
            each = 2 * (NT - 1)
            return m * each + A_AHEAD * (NT - each)

        SIDE = {
            "a": ["xt", "qkv0", "qkv1", "qkv2", "qkv3", "wo-", "ot", "fc"],
            "b": ["xt", "qkv0", "qkv1", "qkv2", "qkv3", "wo-", "qt", "ctx0", "ctx1", "ctx2", "att0", "att1",
                  "ot", "fc"],
            None: ["wo-"],
        }
        A_LONE = len(SIDE["a"]) - 1
        A_PERIODS = B - A_AHEAD
        first_side = A_AHEAD * A_LONE
        a_side = first_side + A_LONE
        b_side = a_side + (A_PERIODS - 1) * len(SIDE["a"])
        end_side = b_side + B * len(SIDE["b"])

        def side_number(phase, layer, n, task):
            order = [t for t in SIDE[layer] if t != "wo-" or phase not in ("start", "first")]
            at = order.index(task)
            if phase == "start":
                return n * A_LONE + at
            if phase == "first":
                return first_side + at
            if layer == "a":
                return n * len(order) + (a_side - len(order) + at)
            if layer == "b":
                return n * len(order) + (b_side - B_FROM * len(order) + at)
            return end_side + (n - (B_FROM + B))

        def side_read(layer, n, m, task):
            if task == "wo-":
                return f_x_done, n
            if task[:3] == "qkv":
                return s_qkv_ready, side_seq(layer, m) * NT + (int(task[3]) + 1)
            if task[:3] == "ctx":
                return b_cum_ready, m * (NB - 1) + min(3 * int(task[3]) + 3, NB - 1)
            if task[:3] == "att":
                return s_o_ready, outputs_before("b", m) + (int(task[3]) + 1)
            if task == "qt":
                return b_qt_ready, m + 1
            return {"xt": s_xt_ready, "ot": s_ot_ready}[task], side_seq(layer, m) + 1

        def outputs_before(layer, m):
            return m if layer == "a" else m * 2 + B

        def side_seq(layer, m):
            return m if layer == "a" else m + B

        LOW, HIGH = slice(0, FD), slice(FD, 2 * FD)

        block = ctx.enter_context(nc.Block())

        def tile_of(ap, t, w=P):
            return ap[:, t * w:(t + 1) * w]

        def a_scores_product(engine, dst, t):
            q = s_qkv[:, t, 0:C].rearrange("p (h o d) -> p h o d", h=AH, o=1)
            k = s_qkv[:, t, C:2 * C].rearrange("p (o t d) -> p o t d", o=1, t=AH)
            return engine.tensor_tensor(dst.rearrange("p (h t d) -> p h t d", h=AH, t=AH),
                                        q.to_broadcast([P, AH, AH, AD]), k.to_broadcast([P, AH, AH, AD]), ALU.mult)

        def a_values_product(engine, dst, t):
            w = a_p[:, t * AH:(t + 1) * AH, :].rearrange("p h (o t) -> p h o t", o=1)
            v = s_qkv[:, t, 2 * C:3 * C].rearrange("p (o d t) -> p o d t", o=1, t=AH)
            return engine.tensor_tensor(dst.rearrange("p (h d t) -> p h d t", h=AH, d=AD),
                                        w.to_broadcast([P, AH, AD, AH]), v.to_broadcast([P, AH, AD, AH]), ALU.mult)

        @block.sync
        def _(sp):
            sp.dma_start(x_all[:, 0, :].rearrange("p (t c) -> p t c", t=NT),
                         x_in[0].rearrange("(t p) c -> p t c", p=P)).then_inc(loaded_x, 16)
            for k, w in enumerate((a_wq, a_wk, a_wv, a_wfc)):
                sp.dma_start(raw_sq[:, k, :], w).then_inc(loaded_w, 16)
            sp.dma_start(raw_sq[:, 4:7, :], b_wqkv.rearrange("(k p) c -> p k c", p=P)).then_inc(loaded_w, 16)
            sp.dma_start(raw_sq[:, 7, :], b_wout).then_inc(loaded_w, 16)
            sp.dma_start(x_all[:, 1:B, :].rearrange("p b (t c) -> p b t c", t=NT),
                         x_in[1:B].rearrange("b (t p) c -> p b t c", p=P)).then_inc(loaded_x, 16)
            sp.dma_start(raw_wq, f_wq).then_inc(loaded_f, 16)
            sp.dma_start(raw_wkv, f_wkv).then_inc(loaded_f, 16)
            sp.dma_start(raw_ws[:, :], f_ws).then_inc(loaded_f, 16)
            sp.dma_start(wo[:, :, :], f_wo.rearrange("(p a) d c -> (a d) p c", a=2)).then_inc(loaded_f, 16)
            sp.dma_start(bo[:, :], f_bo).then_inc(loaded_f, 16)
            with sp.Fori(0, B) as b:
                sp.wait_ge(f_x_done, b + (B + 1))
                sp.dma_start(out[bass.ds(b, 1)].rearrange("b (t p) c -> p (b t) c", p=P),
                             x_all[:, bass.ds(b + B, 1), :].rearrange("p b (t c) -> p (b t) c", t=NT)
                             ).then_inc(stored, 16)
            sp.wait_ge(stored, 16 * B)

        @block.gpsimd
        def _(pool):
            links = [0]

            def link(ins):
                links[0] += 1
                ins.then_inc(p_chain, 1)
                pool.wait_ge(p_chain, links[0])

            link(nc.gpsimd.memset(ident[:, :], 0.0))
            nc.gpsimd.affine_select(out=ident[:, :], in_=ident[:, :], compare_op=ALU.not_equal, fill=1.0,
                                    base=0, pattern=[[-1, P]], channel_multiplier=1).then_inc(ident_done, 1)
            nc.gpsimd.memset(minus_half[:, :], -0.5).then_inc(masks_done, 1)
            link(nc.gpsimd.memset(ctx_mask[:, :], 1.0))
            for view, width in ((ctx_mask[:, 0:C], AD), (ctx_mask[:, C:CW], 1)):
                v = view.rearrange("p (h d) -> p h d", d=width)
                link(nc.gpsimd.affine_select(out=v, in_=v, compare_op=ALU.is_ge, fill=0.0, base=0,
                                             pattern=[[-AD, AH], [0, width]], channel_multiplier=1))
                link(nc.gpsimd.affine_select(out=v, in_=v, compare_op=ALU.is_ge, fill=0.0, base=AD - 1,
                                             pattern=[[AD, AH], [0, width]], channel_multiplier=-1))
            link(nc.gpsimd.memset(before[:, :, :], 1.0))
            link(nc.gpsimd.memset(after[:, :, :], 1.0))
            nc.gpsimd.affine_select(out=before[:, :, :], in_=before[:, :, :], compare_op=ALU.is_gt, fill=0.0,
                                    base=0, pattern=[[1, FH], [-1, FH]], channel_multiplier=0)\
                .then_inc(masks_done, 1)
            nc.gpsimd.affine_select(out=after[:, :, :], in_=after[:, :, :], compare_op=ALU.is_gt, fill=0.0,
                                    base=0, pattern=[[-1, FH], [1, FH]], channel_multiplier=0)\
                .then_inc(masks_done, 1)
            nc.gpsimd.memset(b_ctx[:, 0, :], 0.0).then_inc(masks_done, 1)
            pool.wait_ge(masks_done, 4)

            def f_rstd_step(n):
                pool.wait_ge(f_var_ready, n + 1)
                nc.gpsimd.tensor_tensor(f_rstd[:, :], f_var[:, :], minus_half[:, :], ALU.pow)\
                    .then_inc(f_rstd_ready, 1)

            def side_rstd_step(layer, m):
                pool.wait_ge(s_var_ready, side_seq(layer, m) + 1)
                nc.gpsimd.tensor_tensor(s_rstd[:, :], s_var[:, :], minus_half[:, :], ALU.pow)\
                    .then_inc(s_rstd_ready, 1)

            def scale_step(n, p):
                pool.wait_ge(recip_ready, n * NP + (p + 1))
                pool.wait_ge(gate_ready, n + 1)
                nc.gpsimd.tensor_tensor(
                    scale_w[:, :, :, :],
                    gate[:, :, 2 * p:2 * p + 2].rearrange("p t (a o) -> p t a o", o=1).to_broadcast([P, NT, 2, FD]),
                    recip[:, :, :].rearrange("p a (t o) -> p t a o", o=1).to_broadcast([P, NT, 2, FD]),
                    ALU.mult).then_inc(scale_ready, 1)

            def a_scores_step(phase, m, t):
                pool.wait_ge(s_qkv_ready, m * NT + (t + 1))
                pool.wait_ge(a_prod_used, pool_products(phase, m) + (t + 1))
                a_scores_product(nc.gpsimd, a_prod[:, t % 2, :], t).then_inc(a_prod_ready, 1)

            def a_values_step(phase, m, t):
                if t == 0:
                    pool.wait_ge(a_p_ready, m + 1)
                k = pool_tiles(phase) + t
                pool.wait_ge(a_prod_used, pool_products(phase, m) + (k + 1))
                a_values_product(nc.gpsimd, a_prod[:, k % 2, :], t).then_inc(a_prod_ready, 1)

            def b_mask_step(m, n):
                pool.wait_ge(b_cum_ready, m * (NB - 1) + n)
                nc.gpsimd.tensor_tensor(b_ctx[:, n, :], b_cum[:, n, :], ctx_mask[:, :], ALU.mult)\
                    .then_inc(b_ctx_ready, 1)

            def period(phase, n, layer, m):
                if phase != "first":
                    scale_step(n - 1, NP - 1)
                if layer == "a":
                    side_rstd_step("a", m)
                    a_scores_step(phase, m, 0)
                    a_scores_step(phase, m, 1)
                    scale_step(n, 0)
                    a_scores_step(phase, m, 2)
                    f_rstd_step(n + 1)
                    a_values_step(phase, m, 0)
                    scale_step(n, 1)
                    a_values_step(phase, m, 1)
                    a_values_step(phase, m, 2)
                    scale_step(n, 2)
                    return
                if layer == "b":
                    side_rstd_step("b", m)
                scale_step(n, 0)
                if phase != "last":
                    f_rstd_step(n + 1)
                scale_step(n, 1)
                if layer == "b":
                    for k in range(1, NB):
                        b_mask_step(m, k)
                scale_step(n, 2)

            def tail():
                scale_step(LAST, NP - 1)

            for m in range(A_AHEAD):
                side_rstd_step("a", m)
                for t in range(pool_tiles("start")):
                    a_scores_step("start", m, t)
                for t in range(pool_tiles("start")):
                    a_values_step("start", m, t)
            f_rstd_step(0)
            period("first", 0, "a", A_AHEAD)
            with pool.Fori(1, A_PERIODS) as n:
                period("loop", n, "a", n + A_AHEAD)
            with pool.Fori(0, B) as m:
                period("loop", m + B_FROM, "b", m)
            period("loop", LAST - 1, None, 0)
            period("last", LAST, None, 0)
            tail()

        @block.scalar
        def _(act):
            act.wait_ge(ones_done, 2)
            act.wait_ge(loaded_f, 5 * 16)
            nc.scalar.activation(w_hi[:, 0:FC], raw_wq, ACT.Copy, scale=F_SCALE).then_inc(w_hi_done, 1)
            nc.scalar.activation(w_hi[:, FC:3 * FC], raw_wkv, ACT.Copy).then_inc(w_hi_done, 1)
            nc.scalar.activation(ws_hi[:, :], raw_ws[:, :], ACT.Copy).then_inc(w_hi_done, 1)

            def misc_step(phase, n, task):
                act.wait_ge(misc_full, misc_number(phase, n, task) + 1)
                name = seq_of(n, task)[1]
                if name == "xt":
                    nc.scalar.activation(xt_hi[:, :], misc[:, :], ACT.Copy).then_inc(xt_hi_ready, 1)
                if name == "logits":
                    nc.scalar.activation(g_exp[:, :, :], misc[:, 0:NT * FH].rearrange("p (t h) -> p t h", t=NT),
                                         ACT.Exp, scale=-1.0).then_inc(gate_exp_ready, 1)
                if name == "gate_t":
                    nc.scalar.activation(gate_t[:, :], misc[0:FH, :], ACT.Copy).then_inc(gate_t_ready, 1)
                if name[:5] == "scale":
                    nc.scalar.activation(scale_t[:, :], misc[:, :], ACT.Copy).then_inc(scale_t_ready, 1)
                if name[0] == "v":
                    nc.scalar.activation(v_sb[:, int(name[1]), :], misc[:, :], ACT.Copy).then_inc(v_ready, 1)
                if name[0] == "q":
                    p = int(name[1]) % 2
                    nc.scalar.activation(q_both[LOW, p, 0, :], misc[LOW, :], ACT.Copy)
                    nc.scalar.activation(q_both[HIGH, p, 1, :], misc[HIGH, :], ACT.Copy).then_inc(qk_hi_ready, 1)
                if name[0] == "k":
                    p = int(name[1]) % 2
                    nc.scalar.activation(k_hi[:, p, :], misc[:, :], ACT.Copy)
                    nc.scalar.activation(k_cross[HIGH, p, 0, :], misc[LOW, :], ACT.Copy)
                    nc.scalar.activation(k_cross[LOW, p, 1, :], misc[HIGH, :], ACT.Copy).then_inc(qk_hi_ready, 1)

            def side_filled(phase, layer, n, task):
                act.wait_ge(side_full, side_number(phase, layer, n, task) + 1)

            def exp_step(n, u):
                act.wait_ge(max_ready, n * UNITS + (u + 1))
                nc.scalar.activation(probs[:, u % 4, :], scores[u % 3][:, :], ACT.Exp,
                                     bias=neg_max[:, u:u + 1], accum_out=row_sum[:, u:u + 1]).then_inc(exp_done, 1)

            def move_step(n, u):
                act.wait_ge(turned_ready, n * UNITS + (u + 1))
                h, t = u // NT, u % NT
                nc.scalar.activation(probs_t[:, h % 4, :, t * P:(t + 1) * P],
                                     turned[u % 2][:, :].rearrange("p (c q) -> p c q", c=NT), ACT.Copy)\
                    .then_inc(moved, 1)

            def side_xt(phase, layer, n, m):
                side_filled(phase, layer, n, "xt")
                nc.scalar.activation(s_xt[:, :], side[:, :], ACT.Copy).then_inc(s_xt_ready, 1)

            def side_qkv(phase, layer, n, m, t):
                side_filled(phase, layer, n, f"qkv{t}")
                nc.scalar.activation(s_qkv[:, t, 0:3 * C], side[:, 0:3 * C], ACT.Copy).then_inc(s_qkv_ready, 1)

            def side_ot(phase, layer, n, m):
                side_filled(phase, layer, n, "ot")
                nc.scalar.activation(s_ot[:, :], side[:, :], ACT.Copy).then_inc(s_ot_ready, 1)

            def a_exp(m):
                act.wait_ge(a_s_ready, m + 1)
                nc.scalar.activation(a_p[:, :, :], a_s[:, :, :], ACT.Exp, scale=A_SCALE).then_inc(a_p_ready, 1)

            def b_exp(m):
                act.wait_ge(b_q_ready, m + 1)
                nc.scalar.activation(b_e[:, :, :], b_q[:, :, :], ACT.Exp).then_inc(b_e_ready, 1)
                for k in range(2):
                    rows = slice(k * BUCKET, (k + 1) * BUCKET)
                    nc.scalar.activation(b_k[rows, k, :, :], s_qkv[rows, :, C:2 * C], ACT.Exp).then_inc(b_k_ready, 1)

            def b_qt_step(phase, n, m):
                side_filled(phase, "b", n, "qt")
                nc.scalar.activation(b_qt[:, :], side[:, :], ACT.Copy).then_inc(b_qt_ready, 1)

            def side_slot(phase, layer, n, m, u):
                if not layer:
                    return
                if u == SIDE_XT:
                    side_xt(phase, layer, n, m)
                if 0 <= u - SIDE_QKV < NT:
                    side_qkv(phase, layer, n, m, u - SIDE_QKV)
                if layer == "a":
                    if u == A_EXP:
                        a_exp(m)
                    if u == A_OT:
                        side_ot(phase, "a", n, m)
                else:
                    if u == B_EXP:
                        b_exp(m)
                    if u == B_QT:
                        b_qt_step(phase, n, m)
                    if u == B_OT:
                        side_ot(phase, "b", n, m)

            def period(phase, n, layer, m):
                for u in range(UNITS):
                    if u in MISC_SLOTS and runs(phase, MISC_SLOTS[u]):
                        misc_step(phase, n, MISC_SLOTS[u])
                    side_slot(phase, layer, n, m, u - 1)
                    move_step(n, u)
                    if u + 2 < UNITS:
                        exp_step(n, u + 2)
                    elif phase != "last":
                        exp_step(n + 1, u + 2 - UNITS)

            def tail():
                misc_step("tail", PERIODS, "scale3-")

            for m in range(A_AHEAD):
                side_xt("start", "a", m, m)
                for t in range(NT):
                    side_qkv("start", "a", m, m, t)
                a_exp(m)
                side_ot("start", "a", m, m)
            for task in ORDER["start"]:
                misc_step("start", -1, task)
            exp_step(0, 0)
            exp_step(0, 1)
            period("first", 0, "a", A_AHEAD)
            with act.Fori(1, A_PERIODS) as n:
                period("loop", n, "a", n + A_AHEAD)
            with act.Fori(0, B) as m:
                period("loop", m + B_FROM, "b", m)
            period("loop", LAST - 1, None, 0)
            period("last", LAST, None, 0)
            tail()

        F_LINKS = 8
        START_LINKS = 4 + NT
        A_LINKS = 4 + 2
        B_LINKS = 9

        @block.vector
        def _(dve):
            dve.sem_inc(a_prod_used, 2)
            dve.sem_inc(b_x_done, 1)
            nc.vector.memset(s_qkv[:, :, 3 * C:3 * C + AH], 1.0).then_inc(ones_done, 1)

            nc.vector.memset(b_k[:, :, :, :], 0.0).then_inc(ones_done, 1)

            dve.wait_ge(w_turned, 1)
            nc.vector.tensor_copy(a_w[:, 0:2 * C], scores[0][:, 0:2 * C]).then_inc(w_copied, 1)
            nc.vector.tensor_copy(a_w[:, 2 * C:3 * C].rearrange("p (d t) -> p d t", d=AD),
                                  scores[0][:, 2 * C:3 * C].rearrange("p (t d) -> p d t", d=AD)).then_inc(w_copied, 1)
            nc.vector.tensor_copy(a_fc[:, :], scores[0][:, 3 * C:4 * C]).then_inc(w_copied, 1)
            nc.vector.tensor_copy(b_w[:, :], scores[1][:, 0:3 * C]).then_inc(w_copied, 1)
            nc.vector.tensor_copy(b_out[:, :], scores[1][:, 3 * C:4 * C]).then_inc(w_copied, 1)

            def split_weights():
                dve.wait_ge(w_hi_done, 3)
                nc.vector.scalar_tensor_tensor(out=w_lo[:, 0:FC], in0=raw_wq, scalar=F_SCALE,
                                               in1=w_hi[:, 0:FC].bitcast(fp32), op0=ALU.mult, op1=ALU.subtract)\
                    .then_inc(w_lo_done, 1)
                nc.vector.tensor_tensor(w_lo[:, FC:3 * FC], raw_wkv, w_hi[:, FC:3 * FC].bitcast(fp32),
                                        ALU.subtract).then_inc(w_lo_done, 1)
                nc.vector.tensor_tensor(ws_lo[:, :], raw_ws[:, :], ws_hi[:, :].bitcast(fp32), ALU.subtract)\
                    .then_inc(w_lo_done, 1)

            class Links:

                def __init__(self, sem, base, count):
                    self.sem, self.base, self.count, self.k = sem, base, count, 0

                def link(self, ins):
                    self.k += 1
                    ins.then_inc(self.sem, 1)
                    dve.wait_ge(self.sem, self.base + self.k)

                def end(self):
                    assert self.k == self.count, (self.k, self.count)

            def side_filled(phase, layer, n, task):
                dve.wait_ge(side_full, side_number(phase, layer, n, task) + 1)

            def norm_step(links, slot, stats, mv, var, ready):
                for t in range(NT):
                    last = nc.vector.bn_stats(stats[:, t, :],
                                              x_all[:, bass.ds(slot, 1), t * C:(t + 1) * C].rearrange("p o c -> p (o c)"))
                links.link(last)
                dve.nop(nofuse=True)
                for t in range(NT):
                    last = nc.vector.bn_aggr(mv[:, t, :], stats[:, t, :])
                links.link(last)
                nc.vector.tensor_scalar(var[:, :], mv[:, :, 1], EPS, None, ALU.add).then_inc(ready, 1)

            def xn_step(slot, mv, rstd, xn, ready):
                for t in range(NT):
                    last = nc.vector.tensor_scalar(
                        xn[:, t, :], x_all[:, bass.ds(slot, 1), t * C:(t + 1) * C].rearrange("p o c -> p (o c)"),
                        mv[:, t, 0:1], rstd[:, t:t + 1], ALU.subtract, ALU.mult)
                last.then_inc(ready, 1)

            def f_norm(links, n, first):
                if first:
                    dve.wait_ge(a_x_done, n + 1)
                else:
                    dve.wait_ge(a_x_done, B)
                    dve.wait_ge(b_x_done, n - (B - 2))
                norm_step(links, n, f_stats, f_mv, f_var, f_var_ready)

            def f_xn_step(n):
                dve.wait_ge(f_rstd_ready, n + 1)
                xn_step(n, f_mv, f_rstd, f_xn, f_xn_ready)

            def lower_parts(n, task):
                s, name = seq_of(n, task)
                if name == "xt":
                    dve.wait_ge(xt_hi_ready, s + 1)
                    nc.vector.tensor_tensor(xt_lo[:, :], misc[:, :], xt_hi[:, :].bitcast(fp32), ALU.subtract)\
                        .then_inc(xt_lo_ready, 1)
                    return
                if name[0] not in "qk":
                    return
                p = int(name[1])
                dve.wait_ge(qk_hi_ready, s * 2 * NP + (2 * p + (name[0] == "k") + 1))
                for a, (own, other) in enumerate(((LOW, HIGH), (HIGH, LOW))):
                    if name[0] == "q":
                        last = nc.vector.tensor_tensor(q_both[other, p % 2, a, :], misc[own, :],
                                                       q_both[own, p % 2, a, :].bitcast(fp32), ALU.subtract)
                    else:
                        last = nc.vector.tensor_tensor(k_cross[own, p % 2, a, :], misc[own, :],
                                                       k_hi[own, p % 2, :].bitcast(fp32), ALU.subtract)
                last.then_inc(qk_lo_ready, 1)

            def gate_step(links, n):
                dve.wait_ge(gate_exp_ready, n + 1)
                links.link(nc.vector.tensor_scalar(g_den[:, :, :], g_exp[:, :, :], 1.0, None, ALU.add))
                links.link(nc.vector.reciprocal(g_sig[:, :, :], g_den[:, :, :]))
                mine = g_sig[:, :, :].rearrange("p t (h o) -> p t h o", o=1).to_broadcast([P, NT, FH, FH])
                other = g_sig[:, :, :].rearrange("p t (o h) -> p t o h", o=1).to_broadcast([P, NT, FH, FH])
                nc.vector.tensor_tensor(g_gt[:, :, :, :], other, mine, ALU.is_gt)
                links.link(nc.vector.tensor_tensor(g_ge[:, :, :, :], other, mine, ALU.is_ge))

                def over_tiles(m):
                    return m[:, :, :].rearrange("p h (o k) -> p o h k", o=1).to_broadcast([P, NT, FH, FH])

                nc.vector.tensor_tensor(g_gt[:, :, :, :], g_gt[:, :, :, :], over_tiles(after), ALU.mult)
                links.link(nc.vector.tensor_tensor(g_ge[:, :, :, :], g_ge[:, :, :, :], over_tiles(before), ALU.mult))
                links.link(nc.vector.tensor_tensor(g_ge[:, :, :, :], g_ge[:, :, :, :], g_gt[:, :, :, :], ALU.add))
                links.link(nc.vector.reduce_sum(g_rank[:, :, :], g_ge[:, :, :, :], AX.X))
                nc.vector.scalar_tensor_tensor(out=gate[:, :, :], in0=g_rank[:, :, :], scalar=TOPK - 0.5,
                                               in1=g_sig[:, :, :], op0=ALU.is_lt, op1=ALU.mult)\
                    .then_inc(gate_ready, 1)

            def max_step(n, u):
                dve.wait_ge(scores_ready, n * UNITS + (u + 1))
                nc.vector.tensor_reduce(neg_max[:, u:u + 1], scores[u % 3][:, :], AX.X, ALU.max, negate=True)\
                    .then_inc(max_ready, 1)

            def recip_step(n, p):
                dve.wait_ge(exp_done, n * UNITS + PAIR * (p + 1))
                nc.vector.reciprocal(recip[:, :, :], row_sum[:, PAIR * p:PAIR * (p + 1)]
                                     .rearrange("p (a t) -> p a t", a=2)).then_inc(recip_ready, 1)

            def out_step(n, p):
                dve.wait_ge(heads_ready, n * NP + (p + 1))
                dve.wait_ge(scale_t_ready, n * NP + (p + 1))
                nc.vector.tensor_tensor(out_t[:, p, :], heads_out[:, :], scale_t[:, :], ALU.mult)\
                    .then_inc(heads_scaled, 1)

            def add_step(dst, src, bank_ap, done):
                nc.vector.tensor_tensor(x_all[:, bass.ds(dst, 1), :].rearrange("p o c -> p (o c)"), bank_ap,
                                        x_all[:, bass.ds(src, 1), :].rearrange("p o c -> p (o c)"), ALU.add)\
                    .then_inc(done, 1)

            def wo_step(phase, layer, n):
                side_filled(phase, layer, n, "wo-")
                add_step(n - 1, n - 1, side[:, :], f_x_done)

            def a_norm(links, m, wait_load):
                if wait_load:
                    dve.wait_ge(loaded_x, 16 if m == 0 else 32)
                norm_step(links, m, s_stats, s_mv, s_var, s_var_ready)

            def side_xn(layer, m):
                dve.wait_ge(s_rstd_ready, side_seq(layer, m) + 1)
                xn_step(m, s_mv, s_rstd, s_xn, s_xn_ready)

            def own_sums(phase, m):
                return m * NT if phase == "start" else m * 2 + A_AHEAD * (NT - 2)

            def own_free(phase, m, k):
                if phase != "start" or m or k:
                    dve.wait_ge(a_own_summed, own_sums(phase, m) + k)

            def a_scores_sum(phase, links, m, t):
                if t < pool_tiles(phase):
                    dve.wait_ge(a_prod_ready, pool_products(phase, m) + (t + 1))
                    src = a_prod[:, t % 2, :]
                else:
                    dve.wait_ge(s_qkv_ready, m * NT + (t + 1))
                    own_free(phase, m, t - pool_tiles(phase))
                    links.link(a_scores_product(nc.vector, a_own[:, :], t))
                    src = a_own[:, :]
                ins = nc.vector.reduce_sum(a_s[:, t * AH:(t + 1) * AH, :],
                                           src.rearrange("p (h t d) -> p h t d", h=AH, t=AH), AX.X)
                if t < pool_tiles(phase):
                    ins.then_inc(a_prod_used, 1)
                else:
                    ins.then_inc(a_own_summed, 1)

            def a_softmax(phase, links, m):
                k = pool_tiles(phase)
                dve.wait_ge(a_prod_used, pool_products(phase, m) + (k + 2))
                dve.wait_ge(a_own_summed, own_sums(phase, m) + (NT - k))
                links.link(nc.vector.reduce_max(a_max[:, :], a_s[:, :, :], AX.X))
                nc.vector.tensor_tensor(a_s[:, :, :], a_s[:, :, :],
                                        a_max[:, :].rearrange("p (h o) -> p h o", o=1)
                                        .to_broadcast([P, NT * AH, AH]), ALU.subtract).then_inc(a_s_ready, 1)

            def a_sums(links, m):
                dve.wait_ge(a_p_ready, m + 1)
                links.link(nc.vector.reduce_sum(a_sum[:, :], a_p[:, :, :], AX.X))
                nc.vector.reciprocal(a_rec[:, :], a_sum[:, :])

            def a_values_sum(phase, links, m, t):
                if t < pool_tiles(phase):
                    k = pool_tiles(phase) + t
                    dve.wait_ge(a_prod_ready, pool_products(phase, m) + (k + 1))
                    src = a_prod[:, k % 2, :]
                else:
                    own_free(phase, m, NT - 2 * pool_tiles(phase) + t)
                    links.link(a_values_product(nc.vector, a_own[:, :], t))
                    src = a_own[:, :]
                ins = nc.vector.reduce_sum(s_o[:, t, :].rearrange("p (h d) -> p h d", h=AH),
                                           src.rearrange("p (h d t) -> p h d t", h=AH, d=AD), AX.X)
                if t < pool_tiles(phase):
                    ins.then_inc(a_prod_used, 1)
                else:
                    ins.then_inc(a_own_summed, 1)

            def a_normalise(phase, m):
                k = pool_tiles(phase)
                dve.wait_ge(a_prod_used, pool_products(phase, m) + (2 * k + 2))
                dve.wait_ge(a_own_summed, own_sums(phase, m) + 2 * (NT - k))
                o = s_o[:, :, :].rearrange("p t (h d) -> p (t h) d", d=AD)
                nc.vector.tensor_tensor(o, o, a_rec[:, :].rearrange("p (h o) -> p h o", o=1)
                                        .to_broadcast([P, NT * AH, AD]), ALU.mult).then_inc(s_o_ready, 1)

            def side_add(phase, layer, n, m):
                side_filled(phase, layer, n, "fc")
                if layer == "a":
                    add_step(m, m, side[:, :], a_x_done)
                else:
                    add_step(m + B, m, side[:, :], b_x_done)

            def b_norm(links, m):
                dve.wait_ge(f_x_done, m + 1)
                norm_step(links, m, s_stats, s_mv, s_var, s_var_ready)

            def b_query_max(links, m):
                dve.wait_ge(s_qkv_ready, (m + (B + 1)) * NT)
                q = s_qkv[:, :, 0:C].rearrange("p t (h d) -> p t h d", d=AD)
                top = a_max[:, :].rearrange("p (t h) -> p t h", t=NT)
                links.link(nc.vector.reduce_max(top, q, AX.X))
                nc.vector.tensor_tensor(b_q[:, :, :].rearrange("p t (h d) -> p t h d", d=AD), q,
                                        top.rearrange("p t (h o) -> p t h o", o=1).to_broadcast([P, NT, AH, AD]),
                                        ALU.subtract).then_inc(b_q_ready, 1)

            def b_query_softmax(links, m):
                dve.wait_ge(b_e_ready, m + 1)
                e = b_e[:, :, :].rearrange("p t (h d) -> p (t h) d", d=AD)
                links.link(nc.vector.reduce_sum(a_sum[:, :], e, AX.X))
                links.link(nc.vector.reciprocal(a_rec[:, :], a_sum[:, :]))
                nc.vector.scalar_tensor_tensor(
                    out=b_q[:, :, :].rearrange("p t (h d) -> p (t h) d", d=AD), in0=e, scalar=A_SCALE,
                    in1=a_rec[:, :].rearrange("p (h o) -> p h o", o=1).to_broadcast([P, NT * AH, AD]),
                    op0=ALU.mult, op1=ALU.mult).then_inc(b_qn_ready, 1)

            def b_sums(phase, n, m, g):
                side_filled(phase, "b", n, f"ctx{g}")
                for k in range(3 * g, min(3 * g + 3, NB - 1)):
                    j = (k - 3 * g) * CW
                    if k == 0:
                        ins = nc.vector.tensor_copy(b_cum[:, 1, :], side[:, 0:CW])
                    else:
                        dve.wait_ge(b_cum_ready, m * (NB - 1) + k)
                        ins = nc.vector.tensor_tensor(b_cum[:, k + 1, :], side[:, j:j + CW], b_cum[:, k, :], ALU.add)
                    ins.then_inc(b_cum_ready, 1)

            def b_attend(phase, links, n, m, g):
                side_filled(phase, "b", n, f"att{g}")
                a = side[:, 0:2 * CW].rearrange("p (t c) -> p t c", t=2)
                links.link(nc.vector.tensor_scalar(b_den[:, :, :], a[:, :, C:CW], 1e-6, None, ALU.max))
                links.link(nc.vector.reciprocal(b_inv[:, :, :], b_den[:, :, :]))
                nc.vector.tensor_tensor(
                    s_o[:, 2 * g:2 * g + 2, :].rearrange("p t (h d) -> p t h d", d=AD),
                    a[:, :, 0:C].rearrange("p t (h d) -> p t h d", d=AD),
                    b_inv[:, :, :].rearrange("p t (h o) -> p t h o", o=1).to_broadcast([P, 2, AH, AD]),
                    ALU.mult).then_inc(s_o_ready, 1)

            def side_slot(phase, layer, links, n, m, u):
                if layer == "a":
                    if u == SIDE_NORM:
                        a_norm(links, m, False)
                    if u == SIDE_XN:
                        side_xn("a", m)
                    if u in A_SCORES_SLOTS:
                        a_scores_sum(phase, links, m, A_SCORES_SLOTS.index(u))
                    if u == A_SOFTMAX:
                        a_softmax(phase, links, m)
                    if u == A_SUMS:
                        a_sums(links, m)
                    if u in A_VALUES_SLOTS:
                        a_values_sum(phase, links, m, A_VALUES_SLOTS.index(u))
                    if u == A_NORMALISE:
                        a_normalise(phase, m)
                    if u == A_FC + 1:
                        side_add(phase, "a", n, m)
                if layer == "b":
                    if u == SIDE_NORM:
                        b_norm(links, m)
                    if u == SIDE_XN:
                        side_xn("b", m)
                    if u == B_MAX:
                        b_query_max(links, m)
                    if u == B_SOFTMAX:
                        b_query_softmax(links, m)
                    if u - 1 in B_CTX:
                        b_sums(phase, n, m, B_CTX.index(u - 1))
                    if u - 1 in B_ATT:
                        b_attend(phase, links, n, m, B_ATT.index(u - 1))
                    if u == B_FC + 1:
                        side_add(phase, "b", n, m)

            def period(phase, n, layer, m):
                links = Links(f_chain, n * F_LINKS + 2, F_LINKS if phase != "last" else F_LINKS - 2)
                a_more = A_AHEAD * (START_LINKS - A_LINKS)
                side_links = Links(s_chain, m * A_LINKS + a_more, A_LINKS) if layer == "a" else \
                    Links(s_chain, m * B_LINKS + (B * A_LINKS + a_more), B_LINKS)
                for u in range(UNITS):
                    if u + 2 < UNITS:
                        max_step(n, u + 2)
                    elif phase != "last":
                        max_step(n + 1, u + 2 - UNITS)
                    if u in RECIP_SLOTS and runs(phase, RECIP_SLOTS[u]):
                        s, p = seq_of(n, RECIP_SLOTS[u])
                        recip_step(s, int(p))
                    if u in MISC_SLOTS and runs(phase, MISC_SLOTS[u]):
                        lower_parts(n, MISC_SLOTS[u])
                    if u - 1 in MISC_SLOTS and MISC_SLOTS[u - 1] == "logits":
                        gate_step(links, n)
                    if u in OUT_SLOTS and runs(phase, OUT_SLOTS[u]):
                        s, p = seq_of(n, OUT_SLOTS[u])
                        out_step(s, int(p))
                    if u - NT in WO_SLOTS and WO_SLOTS[u - NT] == 0 and phase != "first":
                        wo_step(phase, layer, n)
                    if phase != "last":
                        if u == NORM_SLOT:
                            f_norm(links, n + 1, None if layer == "b" else n + 1 < B)
                        if u == XN_SLOT:
                            f_xn_step(n + 1)
                    side_slot(phase, layer, side_links, n, m, u)
                links.end()
                if layer:
                    side_links.end()

            def tail():
                recip_step(LAST, NP - 1)
                out_step(LAST, NP - 1)
                wo_step("tail", None, PERIODS)

            for m in range(A_AHEAD):
                links = Links(s_chain, m * START_LINKS, START_LINKS)
                a_norm(links, m, True)
                side_xn("a", m)
                if m == 0:
                    split_weights()
                for t in (2, 0, 3, 1):
                    a_scores_sum("start", links, m, t)
                a_softmax("start", links, m)
                a_sums(links, m)
                for t in (2, 0, 3, 1):
                    a_values_sum("start", links, m, t)
                a_normalise("start", m)
                side_add("start", "a", m, m)
                links.end()
            links = Links(f_chain, 0, 2)
            dve.wait_ge(masks_done, 4)
            f_norm(links, 0, True)
            f_xn_step(0)
            for task in ORDER["start"]:
                lower_parts(-1, task)
            links.end()
            max_step(0, 0)
            max_step(0, 1)
            period("first", 0, "a", A_AHEAD)
            with dve.Fori(1, A_PERIODS) as n:
                period("loop", n, "a", n + A_AHEAD)
            with dve.Fori(0, B) as m:
                period("loop", m + B_FROM, "b", m)
            period("loop", LAST - 1, None, 0)
            period("last", LAST, None, 0)
            tail()

        @block.tensor
        def _(pe):
            pe.wait_ge(ident_done, 1)
            pe.wait_ge(loaded_w, 6 * 16)
            for k in range(8):
                last = nc.tensor.transpose(tile_of(scores[k // 4], k % 4), raw_sq[:, k, :], ident[:, :])
            last.then_inc(w_turned, 1)
            pe.wait_ge(w_copied, 5)

            def misc_claim(phase, n, task):
                event = misc_before(phase, n, task)
                if event:
                    pe.wait_ge(*event)

            def side_claim(phase, layer, n, m, task):
                order = [t for t in SIDE[layer] if t != "wo-" or phase not in ("start", "first")]
                at = order.index(task)
                if at:
                    pe.wait_ge(*side_read(layer, n, m, order[at - 1]))
                elif task == "wo-":
                    pe.wait_ge(b_x_done, B + 1)
                    pe.wait_ge(f_x_done, n - 1)

            def split_product(dst, l_hi, l_lo, r_hi, r_lo):
                nc.tensor.matmul(dst, l_hi, r_lo, start=True, stop=False)
                nc.tensor.matmul(dst, l_lo, r_hi, start=False, stop=False)
                return nc.tensor.matmul(dst, l_hi, r_hi, start=False, stop=True)

            def misc_step(phase, n, task):
                misc_claim(phase, n, task)
                s, name = seq_of(n, task)
                if name == "xt":
                    pe.wait_ge(f_xn_ready, s + 1)
                    for t in range(NT):
                        last = nc.tensor.transpose(tile_of(misc, t), f_xn[:, t, :], ident[:, :])
                if name == "logits":
                    for t in range(NT):
                        last = split_product(misc[:, t * FH:(t + 1) * FH], tile_of(xt_hi, t), tile_of(xt_lo, t),
                                             ws_hi[:, :], ws_lo[:, :])
                if name == "gate_t":
                    pe.wait_ge(gate_ready, s + 1)
                    for t in range(NT):
                        last = nc.tensor.transpose(misc[0:FH, t * P:(t + 1) * P], gate[:, t, :], ident[:, :])
                if name[:5] == "scale":
                    pe.wait_ge(scale_ready, s * NP + (int(name[5]) + 1))
                    for t in range(NT):
                        last = nc.tensor.transpose(tile_of(misc, t),
                                                   scale_w[:, t, :, :].rearrange("p a d -> p (a d)"), ident[:, :])
                if name[0] == "v":
                    t = int(name[1])
                    last = split_product(misc[:, :], tile_of(xt_hi, t), tile_of(xt_lo, t),
                                         w_hi[:, 2 * FC:3 * FC], w_lo[:, 2 * FC:3 * FC])
                if name[0] in "qk":
                    if name == "q0":
                        pe.wait_ge(xt_lo_ready, s + 1)
                    c = (FC if name[0] == "k" else 0) + int(name[1]) * P
                    last = split_product(misc[:, :], w_hi[:, c:c + P], w_lo[:, c:c + P], xt_hi[:, :], xt_lo[:, :])
                last.then_inc(misc_full, 1)

            def scores_step(n, u):
                h, t = u // NT, u % NT
                p, r = h // 2, (h % 2) * FD
                if u % PAIR == 0:
                    pe.wait_ge(qk_lo_ready, n * 2 * NP + (2 * p + 2))
                if u >= 3:
                    pe.wait_ge(exp_done, n * UNITS + (u - 2))
                q = slice(t * P, (t + 1) * P)
                dst = scores[u % 3][:, :]
                nc.tensor.matmul(dst, q_both[:, p % 2, h % 2, q], k_cross[:, p % 2, h % 2, :], start=True, stop=False)
                nc.tensor.matmul(dst, q_both[r:r + FD, p % 2, h % 2, q], k_hi[r:r + FD, p % 2, :],
                                 start=False, stop=True).then_inc(scores_ready, 1)

            def turn_step(phase, n, u):
                pe.wait_ge(exp_done, n * UNITS + (u + 1))
                if u >= 2 or phase != "first":
                    pe.wait_ge(moved, n * UNITS + (u - 1))
                for c in range(NT):
                    last = nc.tensor.transpose(tile_of(turned[u % 2], c), probs[:, u % 4, c * P:(c + 1) * P],
                                               ident[:, :])
                last.then_inc(turned_ready, 1)

            def pv_step(phase, n, pair, c):
                s, p = seq_of(n, pair)
                p = int(p)
                if c == 0:
                    pe.wait_ge(moved, s * UNITS + PAIR * (p + 1))
                    if p or phase != "first":
                        pe.wait_ge(heads_scaled, s * NP + p)
                if p == 0:
                    pe.wait_ge(v_ready, s * NT + (c + 1))
                for a in range(2):
                    h = 2 * p + a
                    last = nc.tensor.matmul(heads_out[a * FD:(a + 1) * FD, :], v_sb[:, c, h * FD:(h + 1) * FD],
                                            probs_t[:, h % 4, c, :], start=(c == 0), stop=(c == NT - 1))
                if c == NT - 1:
                    last.then_inc(heads_ready, 1)

            def wo_step(phase, layer, n, m, t):
                if t == 0:
                    side_claim(phase, layer, n, m, "wo-")
                    pe.wait_ge(gate_t_ready, n)
                    pe.wait_ge(heads_scaled, n * NP)
                nc.tensor.matmul(tile_of(side, t), gate_t[:, t * P:(t + 1) * P], bo[:, :], start=True, stop=False)
                for p in range(NP):
                    last = nc.tensor.matmul(tile_of(side, t), out_t[:, p, t * P:(t + 1) * P], wo[:, p, :],
                                            start=False, stop=(p == NP - 1))
                if t == NT - 1:
                    last.then_inc(side_full, 1)

            def side_turn(phase, layer, n, m, task, ready, value, src):
                side_claim(phase, layer, n, m, task)
                pe.wait_ge(ready, value)
                for t in range(NT):
                    last = nc.tensor.transpose(tile_of(side, t), src[:, t, :], ident[:, :])
                last.then_inc(side_full, 1)

            def side_xt(phase, layer, n, m):
                side_turn(phase, layer, n, m, "xt", s_xn_ready, side_seq(layer, m) + 1, s_xn)

            def side_qkv(phase, layer, n, m, t):
                side_claim(phase, layer, n, m, f"qkv{t}")
                if t == 0:
                    pe.wait_ge(s_xt_ready, side_seq(layer, m) + 1)
                w = a_w if layer == "a" else b_w
                nc.tensor.matmul(side[:, 0:3 * C], tile_of(s_xt, t), w[:, :], start=True, stop=True)\
                    .then_inc(side_full, 1)

            def side_ot(phase, layer, n, m):
                side_turn(phase, layer, n, m, "ot", s_o_ready, outputs_before(layer, m) + (1 if layer == "a" else 2), s_o)

            def side_fc(phase, layer, n, m):
                side_claim(phase, layer, n, m, "fc")
                pe.wait_ge(s_ot_ready, side_seq(layer, m) + 1)
                w = a_fc if layer == "a" else b_out
                for t in range(NT):
                    last = nc.tensor.matmul(tile_of(side, t), tile_of(s_ot, t), w[:, :], start=True, stop=True)
                last.then_inc(side_full, 1)

            def b_context(phase, n, m, g):
                side_claim(phase, "b", n, m, f"ctx{g}")
                if g == 0:
                    pe.wait_ge(b_k_ready, m * 2 + 2)
                for k in range(3 * g, min(3 * g + 3, NB - 1)):
                    j, t = (k - 3 * g) * CW, k // 2
                    last = nc.tensor.matmul(side[:, j:j + CW], b_k[:, k % 2, t, :],
                                            s_qkv[:, t, 2 * C:2 * C + CW], start=True, stop=True)
                last.then_inc(side_full, 1)

            def b_attend(phase, n, m, g):
                side_claim(phase, "b", n, m, f"att{g}")
                if g == 0:
                    pe.wait_ge(b_qt_ready, m + 1)
                pe.wait_ge(b_ctx_ready, m * (NB - 1) + (3 if g == 0 else NB - 1))
                for k in range(4 * g, 4 * g + 4):
                    r, j = (k % 2) * BUCKET, (k // 2 - 2 * g) * CW
                    last = nc.tensor.matmul(side[r:r + BUCKET, j:j + CW], b_qt[:, k * BUCKET:(k + 1) * BUCKET],
                                            b_ctx[:, k, :], start=True, stop=True)
                last.then_inc(side_full, 1)

            def side_slot(phase, layer, n, m, u):
                if not layer:
                    return
                if u == SIDE_XT:
                    side_xt(phase, layer, n, m)
                if 0 <= u - SIDE_QKV < NT:
                    side_qkv(phase, layer, n, m, u - SIDE_QKV)
                if layer == "a":
                    if u == A_OT:
                        side_ot(phase, "a", n, m)
                    if u == A_FC:
                        side_fc(phase, "a", n, m)
                if layer == "b":
                    if u == B_QT:
                        side_turn(phase, "b", n, m, "qt", b_qn_ready, m + 1, b_q)
                    if u in B_CTX:
                        b_context(phase, n, m, B_CTX.index(u))
                    if u in B_ATT:
                        b_attend(phase, n, m, B_ATT.index(u))
                    if u == B_OT:
                        side_ot(phase, "b", n, m)
                    if u == B_FC:
                        side_fc(phase, "b", n, m)

            def period(phase, n, layer, m):
                for u in range(UNITS):
                    if u in MISC_SLOTS and runs(phase, MISC_SLOTS[u]):
                        misc_step(phase, n, MISC_SLOTS[u])
                    if u + 2 < UNITS:
                        scores_step(n, u + 2)
                    turn_step(phase, n, u)
                    if u + 2 >= UNITS and phase != "last":
                        scores_step(n + 1, u + 2 - UNITS)
                    if u in WO_SLOTS and phase != "first":
                        wo_step(phase, layer, n, m, WO_SLOTS[u])
                    if u in PV_SLOTS and runs(phase, PV_SLOTS[u][0]):
                        pv_step(phase, n, *PV_SLOTS[u])
                    side_slot(phase, layer, n, m, u)

            def tail():
                for c in range(NT):
                    pv_step("tail", PERIODS, "3-", c)
                misc_step("tail", PERIODS, "scale3-")
                for t in range(NT):
                    wo_step("tail", None, PERIODS, 0, t)

            for m in range(A_AHEAD):
                side_xt("start", "a", m, m)
                for t in range(NT):
                    side_qkv("start", "a", m, m, t)
                side_ot("start", "a", m, m)
                side_fc("start", "a", m, m)
            pe.wait_ge(w_lo_done, 3)
            for task in ORDER["start"]:
                misc_step("start", -1, task)
            scores_step(0, 0)
            scores_step(0, 1)
            period("first", 0, "a", A_AHEAD)
            with pe.Fori(1, A_PERIODS) as n:
                period("loop", n, "a", n + A_AHEAD)
            with pe.Fori(0, B) as m:
                period("loop", m + B_FROM, "b", m)
            period("loop", LAST - 1, None, 0)
            period("last", LAST, None, 0)
            tail()


_INS = ['L0_attn_a_x', 'L0_attn_a_Wq', 'L0_attn_a_Wk', 'L0_attn_a_Wv', 'L0_attn_a_Wfc', 'L0_attn_b_W_qkv',
        'L0_attn_b_W_out', 'L0_ffn_Wq', 'L0_ffn_Wkv', 'L0_ffn_Ws', 'L0_ffn_Wo', 'L0_ffn_bo']
_OUTS = [((8, 512, 128), 'float32')]


def kernel(**inputs):
    import numpy as _np
    import concourse.bacc as _bacc
    from concourse import mybir as _mybir
    from concourse.bass_utils import run_bass_kernel_spmd as _run

    nc = _bacc.Bacc("TRN2", target_bir_lowering=False, num_devices=1)
    arrays, args = {}, []
    for name in _INS:
        a = _np.ascontiguousarray(inputs[name])
        arrays[f"in_{name}_dram"] = a
        args.append(nc.dram_tensor(f"in_{name}_dram", a.shape, _mybir.dt.from_np(a.dtype), kind="ExternalInput").ap())
    for i, (shape, dtype) in enumerate(_OUTS):
        dt = _mybir.dt.from_np(_np.dtype(dtype))
        args.append(nc.dram_tensor(f"out_{i}_dram", shape, dt, kind="ExternalOutput").ap())
    bass_hybrid_attention_ffn_kernel(nc, *args)
    r = _run(nc, [arrays], core_ids=[0])
    got = tuple(r.results[0][f"out_{i}_dram"] for i in range(len(_OUTS)))
    return got[0]
```

```python
import concourse.bass as bass
from concourse import mybir
from contextlib import ExitStack


def bass_hybrid_attention_ffn_kernel(
    nc: bass.Bass,
    x_in: bass.AP,
    a_wq: bass.AP,
    a_wk: bass.AP,
    a_wv: bass.AP,
    a_wfc: bass.AP,
    b_wqkv: bass.AP,
    b_wout: bass.AP,
    f_wq: bass.AP,
    f_wkv: bass.AP,
    f_ws: bass.AP,
    f_wo: bass.AP,
    f_bo: bass.AP,
    out: bass.AP,
):
    fp32 = mybir.dt.float32
    fp32r = mybir.dt.float32r
    ALU = mybir.AluOpType
    ACT = mybir.ActivationFunctionType
    AX = mybir.AxisListType

    B, T, C = x_in.shape
    P = 128
    NT = T // P
    AH = 16
    AD = C // AH
    FH = f_bo.shape[0]
    FD = f_wo.shape[1]
    FC = FH * FD
    NP = FH // 2
    TOPK = 3
    EPS = 1e-5
    BUCKET = 64
    NB = T // BUCKET
    CW = C + AH
    UNITS = FH * NT
    A_SCALE = float(AD) ** -0.5
    F_SCALE = float(FD) ** -0.5
    PERIODS = 2 * B
    A_AHEAD = 2
    B_FROM = B - A_AHEAD

    ctx = ExitStack()
    with ctx:
        def sb(name, shape, dt=fp32):
            return ctx.enter_context(nc.sbuf_tensor(name, shape, dt))

        def sem(name):
            return ctx.enter_context(nc.semaphore(name))

        x_all = sb("x_all", [P, 2 * B, NT * C])
        ident = sb("ident", [P, P])
        ctx_mask = sb("ctx_mask", [P, CW])
        before = sb("before", [P, FH, FH])
        after = sb("after", [P, FH, FH])
        minus_half = sb("minus_half", [P, NT])
        warm = sb("warm", [P, 1])
        a_w = sb("a_w", [P, 3 * C])
        a_fc = sb("a_fc", [P, C])
        b_w = sb("b_w", [P, 3 * C])
        b_out = sb("b_out", [P, C])
        raw_ws = sb("raw_ws", [P, FH])
        w_hi = sb("w_hi", [P, 3 * FC], fp32r)
        w_lo = sb("w_lo", [P, 3 * FC], fp32r)
        ws_hi = sb("ws_hi", [P, FH], fp32r)
        ws_lo = sb("ws_lo", [P, FH], fp32r)
        wo = sb("wo", [P, NP, C])
        bo = sb("bo", [FH, C])

        f_stats = sb("f_stats", [P, NT, 6])
        f_mv = sb("f_mv", [P, NT, 2])
        f_var = sb("f_var", [P, NT])
        f_rstd = sb("f_rstd", [P, NT])
        f_xn = sb("f_xn", [P, NT, C])
        xt_hi = sb("xt_hi", [P, T], fp32r)
        xt_lo = sb("xt_lo", [P, T], fp32r)
        q_both = sb("q_both", [P, 2, 2, T], fp32r)
        k_hi = sb("k_hi", [P, 2, T], fp32r)
        k_cross = sb("k_cross", [P, 2, 2, T], fp32r)
        v_sb = sb("v_sb", [P, NT, FC])
        neg_max = sb("neg_max", [P, UNITS])
        row_sum = sb("row_sum", [P, UNITS])
        probs = sb("probs", [P, 4, T])
        probs_t = sb("probs_t", [P, 4, NT, T])
        recip = sb("recip", [P, 2, NT])
        scale_w = sb("scale_w", [P, NT, 2, FD])
        scale_t = sb("scale_t", [P, T])
        out_t = sb("out_t", [P, NP, T])
        raw_wq = probs_t[:, 0, 0, :]
        raw_wkv = probs_t[:, 0, 1:3, :].rearrange("p a c -> p (a c)")
        raw_sq = out_t[:, 0:2, :].rearrange("p a (k c) -> p (a k) c", c=C)
        g_exp = sb("g_exp", [P, NT, FH])
        g_den = sb("g_den", [P, NT, FH])
        g_sig = sb("g_sig", [P, NT, FH])
        g_gt = sb("g_gt", [P, NT, FH, FH])
        g_ge = sb("g_ge", [P, NT, FH, FH])
        g_rank = sb("g_rank", [P, NT, FH])
        gate = sb("gate", [P, NT, FH])
        gate_t = sb("gate_t", [FH, T])

        s_stats = sb("s_stats", [P, NT, 6])
        s_mv = sb("s_mv", [P, NT, 2])
        s_var = sb("s_var", [P, NT])
        s_rstd = sb("s_rstd", [P, NT])
        s_xn = sb("s_xn", [P, NT, C])
        s_xt = sb("s_xt", [P, T])
        s_qkv = sb("s_qkv", [P, NT, 3 * C + AH])
        s_qkv_odd = v_sb
        s_ot = sb("s_ot", [P, T])
        s_o = sb("s_o", [P, NT, C])
        a_prod = sb("a_prod", [P, 2, AH * AH * AD])
        a_own = sb("a_own", [P, AH * AH * AD])
        a_s = sb("a_s", [P, NT * AH, AH])
        a_p = sb("a_p", [P, NT * AH, AH])
        a_max = sb("a_max", [P, NT * AH])
        a_sum = sb("a_sum", [P, NT * AH])
        a_rec = sb("a_rec", [P, NT * AH])
        b_q = sb("b_q", [P, NT, C])
        b_e = sb("b_e", [P, NT, C])
        b_k = sb("b_k", [P, 2, NT, C])
        b_cum = a_prod[:, :, :].rearrange("p a n -> p (a n)")[:, 0:NB * CW].rearrange("p (n c) -> p n c", c=CW)
        b_ctx = sb("b_ctx", [P, NB, CW])
        b_qt = sb("b_qt", [P, T])
        b_den = sb("b_den", [P, 2, AH])
        b_inv = sb("b_inv", [P, 2, AH])

        def bank(name):
            return ctx.enter_context(nc.psum_tensor(name, [P, 512], fp32))

        scores = [bank(f"scores{i}") for i in range(3)]
        turned = [bank(f"turned{i}") for i in range(2)]
        heads_out = bank("heads_out")
        misc = bank("misc")
        side = bank("side")

        loaded_first = sem("loaded_first")
        loaded_x = sem("loaded_x")
        loaded_w = sem("loaded_w")
        loaded_f = sem("loaded_f")
        ident_done = sem("ident_done")
        masks_done = sem("masks_done")
        ones_done = sem("ones_done")
        w_turned = sem("w_turned")
        w_copied = sem("w_copied")
        w_hi_done = sem("w_hi_done")
        w_lo_done = sem("w_lo_done")
        f_chain = sem("f_chain")
        s_chain = sem("s_chain")
        p_chain = sem("p_chain")
        f_var_ready = sem("f_var_ready")
        f_rstd_ready = sem("f_rstd_ready")
        f_xn_ready = sem("f_xn_ready")
        xt_hi_ready = sem("xt_hi_ready")
        xt_lo_ready = sem("xt_lo_ready")
        qk_hi_ready = sem("qk_hi_ready")
        qk_lo_ready = sem("qk_lo_ready")
        k_cross_hi_ready = sem("k_cross_hi_ready")
        v_ready = sem("v_ready")
        misc_full = sem("misc_full")
        scores_ready = sem("scores_ready")
        max_ready = sem("max_ready")
        exp_done = sem("exp_done")
        turned_ready = sem("turned_ready")
        moved = sem("moved")
        heads_ready = sem("heads_ready")
        heads_scaled = sem("heads_scaled")
        recip_ready = sem("recip_ready")
        scale_ready = sem("scale_ready")
        scale_t_ready = sem("scale_t_ready")
        gate_exp_ready = sem("gate_exp_ready")
        g_compared = sem("g_compared")
        g_marks_ready = sem("g_marks_ready")
        gate_ready = sem("gate_ready")
        gate_t_ready = sem("gate_t_ready")
        f_x_done = sem("f_x_done")
        side_full = sem("side_full")
        s_var_ready = sem("s_var_ready")
        s_rstd_ready = sem("s_rstd_ready")
        s_xn_ready = sem("s_xn_ready")
        s_xt_ready = sem("s_xt_ready")
        s_qkv_ready = sem("s_qkv_ready")
        s_o_ready = sem("s_o_ready")
        s_ot_ready = sem("s_ot_ready")
        a_prod_ready = sem("a_prod_ready")
        a_prod_used = sem("a_prod_used")
        a_own_summed = sem("a_own_summed")
        a_s_ready = sem("a_s_ready")
        a_p_ready = sem("a_p_ready")
        a_sum_ready = sem("a_sum_ready")
        a_rec_ready = sem("a_rec_ready")
        a_x_done = sem("a_x_done")
        b_q_ready = sem("b_q_ready")
        b_e_ready = sem("b_e_ready")
        b_k_ready = sem("b_k_ready")
        b_qn_ready = sem("b_qn_ready")
        b_qt_ready = sem("b_qt_ready")
        b_cum_ready = sem("b_cum_ready")
        b_ctx_ready = sem("b_ctx_ready")
        b_x_done = sem("b_x_done")
        stored = sem("stored")

        PAIR = 2 * NT
        LAST = PERIODS - 1
        MISC_SLOTS = {0: "q1", 2: "k1", 4: "scale3-", 5: "v0", 6: "v1", 8: "q2", 10: "v2", 11: "v3",
                      12: "k2", 14: "scale0", 16: "gate_t", 17: "q3", 19: "k3", 21: "scale1", 23: "xt+",
                      25: "logits+", 26: "q0+", 28: "k0+", 30: "scale2"}
        PV_SLOTS = {PAIR * p + s: (f"{p - 1}" if p else f"{NP - 1}-", c)
                    for p in range(NP) for c, s in enumerate((1, 2, 3, 4))}
        RECIP_SLOTS = {PAIR * p: (f"{p - 1}" if p else f"{NP - 1}-") for p in range(NP)}
        OUT_SLOTS = {5: "3-", 16: "0", 22: "1", 31: "2"}
        WO_SLOTS = {13: (0, 1), 14: (2,), 15: (3,)}
        WO_ADD = 15
        GATE_SLOTS = (4, 7)
        NORM_SLOT, XN_SLOT = 10, 14
        SIDE_NORM, SIDE_XN, SIDE_XT, SIDE_QKV = 1, 3, 4, (5, 7, 9, 11)
        A_SCORES_SLOTS = (9, 10, 11, 12, 13, 14, 15, 16)
        A_VALUES_SLOTS = (18, 20, 22, 23, 24, 25, 26, 27)
        A_SOFTMAX, A_EXP, A_SUMS, A_RECIP = (12, 19), (14, 20), (16, 23), 25
        A_NORMALISE, A_OT, A_FC, A_ADD = 27, 29, 31, 31
        B_MAX, B_EXP, B_SOFTMAX, B_QT = 13, 12, 14, 16
        B_CTX, B_SUM, B_ATT, B_OUT = (18, 21, 23), (19, 21, 23), (25, 26), (25, 27)
        B_OT, B_FC, B_ADD = 28, 31, 31

        def runs(phase, task):
            if phase == "start":
                return task[-1] == "+"
            return not (phase == "first" and task[-1] == "-" or phase == "last" and task[-1] == "+")

        def seq_of(n, task):
            if task[-1] == "+":
                return n + 1, task[:-1]
            if task[-1] == "-":
                return n - 1, task[:-1]
            return n, task

        ORDER = {ph: [t for t in MISC_SLOTS.values() if runs(ph, t)] for ph in ("start", "first", "loop", "last")}
        ORDER["tail"] = ["scale3-"]

        def misc_number(phase, n, task):
            before_it = ORDER[phase].index(task)
            if phase == "start":
                return before_it
            if phase == "first":
                return len(ORDER["start"]) + before_it
            whole = len(ORDER["loop"])
            shift = len(ORDER["start"]) + len(ORDER["first"]) - whole
            if phase == "tail":
                return (LAST - 1) * whole + len(ORDER["last"]) + shift + whole + before_it
            return n * whole + (shift + before_it)

        def misc_read(n, task):
            s, name = seq_of(n, task)
            if name[0] in "qk":
                return qk_lo_ready, s * 2 * NP + (2 * int(name[1]) + (name[0] == "k") + 1)
            if name[0] == "v":
                return v_ready, s * NT + (int(name[1]) + 1)
            if name[:5] == "scale":
                return scale_t_ready, s * NP + (int(name[5]) + 1)
            return {"gate_t": gate_t_ready, "xt": xt_lo_ready, "logits": gate_exp_ready}[name], s + 1

        def misc_before(phase, n, task):
            at = ORDER[phase].index(task)
            if at:
                return misc_read(n, ORDER[phase][at - 1])
            if phase == "start":
                return None
            return misc_read(n - 1, ORDER["start" if phase == "first" else "loop"][-1])

        def pool_tiles(phase):
            return NT - 1 if phase == "start" else NT

        def pool_products(phase, m):
            if phase == "start":
                return m * 2 * (NT - 1)
            return m * 2 * NT - A_AHEAD * 2

        SIDE = {
            "a": ["xt", "qkv0", "qkv1", "qkv2", "qkv3", "wo-", "ot", "fc"],
            "b": ["xt", "qkv0", "qkv1", "qkv2", "qkv3", "wo-", "qt", "ctx0", "ctx1", "ctx2", "att0", "att1",
                  "ot", "fc"],
            None: ["wo-"],
        }
        A_LONE = len(SIDE["a"]) - 1
        A_PERIODS = B - A_AHEAD
        first_side = A_AHEAD * A_LONE
        a_side = first_side + A_LONE
        b_side = a_side + (A_PERIODS - 1) * len(SIDE["a"])
        end_side = b_side + B * len(SIDE["b"])

        START_SIDE = [(m, task) for m in range(A_AHEAD) for task in SIDE["a"][:5]] + \
                     [(m, task) for m in range(A_AHEAD) for task in ("ot", "fc")]

        def side_number(phase, layer, n, task):
            if phase == "start":
                return START_SIDE.index((n, task))
            order = [t for t in SIDE[layer] if t != "wo-" or phase != "first"]
            at = order.index(task)
            if phase == "first":
                return first_side + at
            if layer == "a":
                return n * len(order) + (a_side - len(order) + at)
            if layer == "b":
                return n * len(order) + (b_side - B_FROM * len(order) + at)
            return end_side + (n - (B_FROM + B))

        def side_read(layer, n, m, task):
            if task == "wo-":
                return f_x_done, n
            if task == "fc":
                return a_x_done, m + 1
            if task[:3] == "qkv":
                return s_qkv_ready, side_seq(layer, m) * NT + (int(task[3]) + 1)
            if task[:3] == "ctx":
                return b_cum_ready, m * (NB - 1) + min(3 * int(task[3]) + 3, NB - 1)
            if task[:3] == "att":
                return s_o_ready, outputs_before("b", m) + (int(task[3]) + 1)
            if task == "qt":
                return b_qt_ready, m + 1
            return {"xt": s_xt_ready, "ot": s_ot_ready}[task], side_seq(layer, m) + 1

        def outputs_before(layer, m):
            return m if layer == "a" else m * 2 + B

        def side_seq(layer, m):
            return m if layer == "a" else m + B

        LOW, HIGH = slice(0, FD), slice(FD, 2 * FD)

        block = ctx.enter_context(nc.Block())

        def tile_of(ap, t, w=P):
            return ap[:, t * w:(t + 1) * w]

        def qkv_bank(phase, t):
            return (side, scores[2], turned[0], turned[1])[t] if phase == "start" else side

        def side_qkv_of(phase, m):
            return s_qkv_odd if phase == "start" and m == 1 else s_qkv

        def a_scores_product(engine, phase, m, dst, t):
            qkv = side_qkv_of(phase, m)
            q = qkv[:, t, 0:C].rearrange("p (h o d) -> p h o d", h=AH, o=1)
            k = qkv[:, t, C:2 * C].rearrange("p (o t d) -> p o t d", o=1, t=AH)
            return engine.tensor_tensor(dst.rearrange("p (h t d) -> p h t d", h=AH, t=AH),
                                        q.to_broadcast([P, AH, AH, AD]), k.to_broadcast([P, AH, AH, AD]), ALU.mult)

        def a_values_product(engine, phase, m, dst, t):
            w = a_p[:, t * AH:(t + 1) * AH, :].rearrange("p h (o t) -> p h o t", o=1)
            v = side_qkv_of(phase, m)[:, t, 2 * C:3 * C].rearrange("p (o d t) -> p o d t", o=1, t=AH)
            return engine.tensor_tensor(dst.rearrange("p (h d t) -> p h d t", h=AH, d=AD),
                                        w.to_broadcast([P, AH, AD, AH]), v.to_broadcast([P, AH, AD, AH]), ALU.mult)

        @block.sync
        def _(sp):
            sp.dma_start(x_all[:, 0, :].rearrange("p (t c) -> p t c", t=NT),
                         x_in[0].rearrange("(t p) c -> p t c", p=P)).then_inc(loaded_first, 16)
            for k, w in enumerate((a_wq, a_wk, a_wv, a_wfc)):
                sp.dma_start(raw_sq[:, k, :], w).then_inc(loaded_w, 16)
            sp.dma_start(raw_sq[:, 4:7, :], b_wqkv.rearrange("(k p) c -> p k c", p=P)).then_inc(loaded_w, 16)
            sp.dma_start(raw_sq[:, 7, :], b_wout).then_inc(loaded_w, 16)
            sp.dma_start(x_all[:, 1:B, :].rearrange("p b (t c) -> p b t c", t=NT),
                         x_in[1:B].rearrange("b (t p) c -> p b t c", p=P)).then_inc(loaded_x, 16)
            sp.dma_start(raw_wq, f_wq).then_inc(loaded_f, 16)
            sp.dma_start(raw_wkv, f_wkv).then_inc(loaded_f, 16)
            sp.dma_start(raw_ws[:, :], f_ws).then_inc(loaded_f, 16)
            sp.dma_start(wo[:, :, :], f_wo.rearrange("(p a) d c -> (a d) p c", a=2)).then_inc(loaded_f, 16)
            sp.dma_start(bo[:, :], f_bo).then_inc(loaded_f, 16)
            with sp.Fori(0, B) as b:
                sp.wait_ge(f_x_done, b + (B + 1))
                sp.dma_start(out[bass.ds(b, 1)].rearrange("b (t p) c -> p (b t) c", p=P),
                             x_all[:, bass.ds(b + B, 1), :].rearrange("p b (t c) -> p (b t) c", t=NT)
                             ).then_inc(stored, 16)
            sp.wait_ge(stored, 16 * B)

        @block.gpsimd
        def _(pool):
            links = [0]

            def link(ins):
                links[0] += 1
                ins.then_inc(p_chain, 1)
                pool.wait_ge(p_chain, links[0])

            link(nc.gpsimd.memset(ident[:, :], 0.0))
            nc.gpsimd.affine_select(out=ident[:, :], in_=ident[:, :], compare_op=ALU.not_equal, fill=1.0,
                                    base=0, pattern=[[-1, P]], channel_multiplier=1).then_inc(ident_done, 1)
            nc.gpsimd.memset(minus_half[:, :], -0.5).then_inc(masks_done, 1)
            pool.wait_ge(masks_done, 1)
            pool.wait_ge(s_var_ready, 1)
            nc.gpsimd.tensor_tensor(s_rstd[:, :], s_var[:, :], minus_half[:, :], ALU.pow).then_inc(s_rstd_ready, 1)
            link(nc.gpsimd.memset(ctx_mask[:, :], 1.0))
            for view, width in ((ctx_mask[:, 0:C], AD), (ctx_mask[:, C:CW], 1)):
                v = view.rearrange("p (h d) -> p h d", d=width)
                link(nc.gpsimd.affine_select(out=v, in_=v, compare_op=ALU.is_ge, fill=0.0, base=0,
                                             pattern=[[-AD, AH], [0, width]], channel_multiplier=1))
                link(nc.gpsimd.affine_select(out=v, in_=v, compare_op=ALU.is_ge, fill=0.0, base=AD - 1,
                                             pattern=[[AD, AH], [0, width]], channel_multiplier=-1))
            link(nc.gpsimd.memset(before[:, :, :], 1.0))
            link(nc.gpsimd.memset(after[:, :, :], 1.0))
            nc.gpsimd.affine_select(out=before[:, :, :], in_=before[:, :, :], compare_op=ALU.is_gt, fill=0.0,
                                    base=0, pattern=[[1, FH], [-1, FH]], channel_multiplier=0)\
                .then_inc(masks_done, 1)
            nc.gpsimd.affine_select(out=after[:, :, :], in_=after[:, :, :], compare_op=ALU.is_gt, fill=0.0,
                                    base=0, pattern=[[-1, FH], [1, FH]], channel_multiplier=0)\
                .then_inc(masks_done, 1)
            nc.gpsimd.memset(b_ctx[:, 0, :], 0.0).then_inc(masks_done, 1)
            pool.wait_ge(masks_done, 4)

            constants = links[0]

            def gate_marks(n):
                pool.wait_ge(g_compared, n + 1)

                def over_tiles(m):
                    return m[:, :, :].rearrange("p h (o k) -> p o h k", o=1).to_broadcast([P, NT, FH, FH])

                nc.gpsimd.tensor_tensor(g_gt[:, :, :, :], g_gt[:, :, :, :], over_tiles(after), ALU.mult)
                nc.gpsimd.tensor_tensor(g_ge[:, :, :, :], g_ge[:, :, :, :], over_tiles(before), ALU.mult)\
                    .then_inc(p_chain, 1)
                pool.wait_ge(p_chain, n + (constants + 1))
                nc.gpsimd.tensor_tensor(g_ge[:, :, :, :], g_ge[:, :, :, :], g_gt[:, :, :, :], ALU.add)\
                    .then_inc(g_marks_ready, 1)

            def f_rstd_step(n):
                pool.wait_ge(f_var_ready, n + 1)
                nc.gpsimd.tensor_tensor(f_rstd[:, :], f_var[:, :], minus_half[:, :], ALU.pow)\
                    .then_inc(f_rstd_ready, 1)

            def side_rstd_step(layer, m):
                pool.wait_ge(s_var_ready, side_seq(layer, m) + 1)
                nc.gpsimd.tensor_tensor(s_rstd[:, :], s_var[:, :], minus_half[:, :], ALU.pow)\
                    .then_inc(s_rstd_ready, 1)

            def scale_step(n, p):
                pool.wait_ge(recip_ready, n * NP + (p + 1))
                pool.wait_ge(gate_ready, n + 1)
                nc.gpsimd.tensor_tensor(
                    scale_w[:, :, :, :],
                    gate[:, :, 2 * p:2 * p + 2].rearrange("p t (a o) -> p t a o", o=1).to_broadcast([P, NT, 2, FD]),
                    recip[:, :, :].rearrange("p a (t o) -> p t a o", o=1).to_broadcast([P, NT, 2, FD]),
                    ALU.mult).then_inc(scale_ready, 1)

            def a_scores_step(phase, m, t):
                pool.wait_ge(s_qkv_ready, m * NT + (t + 1))
                pool.wait_ge(a_prod_used, pool_products(phase, m) + (t + 1))
                a_scores_product(nc.gpsimd, phase, m, a_prod[:, t % 2, :], t).then_inc(a_prod_ready, 1)

            def a_values_step(phase, m, t):
                if t % 2 == 0:
                    pool.wait_ge(a_p_ready, m * 2 + (t // 2 + 1))
                k = pool_tiles(phase) + t
                pool.wait_ge(a_prod_used, pool_products(phase, m) + (k + 1))
                a_values_product(nc.gpsimd, phase, m, a_prod[:, k % 2, :], t).then_inc(a_prod_ready, 1)

            def b_mask_step(m, n):
                pool.wait_ge(b_cum_ready, m * (NB - 1) + n)
                nc.gpsimd.tensor_tensor(b_ctx[:, n, :], b_cum[:, n, :], ctx_mask[:, :], ALU.mult)\
                    .then_inc(b_ctx_ready, 1)

            def period(phase, n, layer, m):
                if layer == "a":
                    if phase != "first":
                        scale_step(n - 1, NP - 1)
                    side_rstd_step("a", m)
                    gate_marks(n)
                    a_scores_step(phase, m, 0)
                    a_scores_step(phase, m, 1)
                    scale_step(n, 0)
                    a_scores_step(phase, m, 2)
                    f_rstd_step(n + 1)
                    a_scores_step(phase, m, 3)
                    a_values_step(phase, m, 0)
                    scale_step(n, 1)
                    a_values_step(phase, m, 1)
                    a_values_step(phase, m, 2)
                    a_values_step(phase, m, 3)
                    scale_step(n, 2)
                    return
                scale_step(n - 1, NP - 1)
                if layer == "b":
                    side_rstd_step("b", m)
                gate_marks(n)
                scale_step(n, 0)
                if phase != "last":
                    f_rstd_step(n + 1)
                scale_step(n, 1)
                if layer == "b":
                    for k in range(1, NB):
                        b_mask_step(m, k)
                scale_step(n, 2)

            def tail():
                scale_step(LAST, NP - 1)

            for m in range(A_AHEAD):
                a_scores_step("start", m, 0)
                a_scores_step("start", m, 1)
                if m == 0:
                    side_rstd_step("a", 1)
                else:
                    f_rstd_step(0)
                a_scores_step("start", m, 2)
                for t in range(pool_tiles("start")):
                    a_values_step("start", m, t)
            period("first", 0, "a", A_AHEAD)
            with pool.Fori(1, A_PERIODS) as n:
                period("loop", n, "a", n + A_AHEAD)
            with pool.Fori(0, B) as m:
                period("loop", m + B_FROM, "b", m)
            period("loop", LAST - 1, None, 0)
            period("last", LAST, None, 0)
            tail()

        @block.scalar
        def _(act):
            act.wait_ge(ident_done, 1)
            nc.scalar.activation(warm[:, :], ident[:, 0:1], ACT.Copy)
            act.wait_ge(ones_done, 2)

            def weights_hi():
                act.wait_ge(loaded_f, 5 * 16)
                nc.scalar.activation(w_hi[:, 0:FC], raw_wq, ACT.Copy, scale=F_SCALE).then_inc(w_hi_done, 1)
                nc.scalar.activation(w_hi[:, FC:3 * FC], raw_wkv, ACT.Copy).then_inc(w_hi_done, 1)
                nc.scalar.activation(ws_hi[:, :], raw_ws[:, :], ACT.Copy).then_inc(w_hi_done, 1)

            def misc_step(phase, n, task):
                act.wait_ge(misc_full, misc_number(phase, n, task) + 1)
                name = seq_of(n, task)[1]
                if name == "xt":
                    nc.scalar.activation(xt_hi[:, :], misc[:, :], ACT.Copy).then_inc(xt_hi_ready, 1)
                if name == "logits":
                    nc.scalar.activation(g_exp[:, :, :], misc[:, 0:NT * FH].rearrange("p (t h) -> p t h", t=NT),
                                         ACT.Exp, scale=-1.0).then_inc(gate_exp_ready, 1)
                if name == "gate_t":
                    nc.scalar.activation(gate_t[:, :], misc[0:FH, :], ACT.Copy).then_inc(gate_t_ready, 1)
                if name[:5] == "scale":
                    nc.scalar.activation(scale_t[:, :], misc[:, :], ACT.Copy).then_inc(scale_t_ready, 1)
                if name[0] == "v":
                    nc.scalar.activation(v_sb[:, int(name[1]), :], misc[:, :], ACT.Copy).then_inc(v_ready, 1)
                if name[0] == "q":
                    p = int(name[1]) % 2
                    nc.scalar.activation(q_both[LOW, p, 0, :], misc[LOW, :], ACT.Copy)
                    nc.scalar.activation(q_both[HIGH, p, 1, :], misc[HIGH, :], ACT.Copy).then_inc(qk_hi_ready, 1)
                if name[0] == "k":
                    p = int(name[1]) % 2
                    nc.scalar.activation(k_hi[:, p, :], misc[:, :], ACT.Copy).then_inc(qk_hi_ready, 1)
                    act.wait_ge(qk_hi_ready, seq_of(n, task)[0] * 2 * NP + (2 * int(name[1]) + 2))
                    nc.scalar.activation(k_cross[HIGH, p, 0, :], k_hi[LOW, p, :], ACT.Copy)
                    nc.scalar.activation(k_cross[LOW, p, 1, :], k_hi[HIGH, p, :], ACT.Copy)\
                        .then_inc(k_cross_hi_ready, 1)

            def side_filled(phase, layer, n, task):
                act.wait_ge(side_full, side_number(phase, layer, n, task) + 1)

            def exp_step(n, u):
                act.wait_ge(max_ready, n * UNITS + (u + 1))
                nc.scalar.activation(probs[:, u % 4, :], scores[u % 3][:, :], ACT.Exp,
                                     bias=neg_max[:, u:u + 1], accum_out=row_sum[:, u:u + 1]).then_inc(exp_done, 1)

            def move_step(n, u):
                act.wait_ge(turned_ready, n * UNITS + (u + 1))
                h, t = u // NT, u % NT
                nc.scalar.activation(probs_t[:, h % 4, :, t * P:(t + 1) * P],
                                     turned[u % 2][:, :].rearrange("p (c q) -> p c q", c=NT), ACT.Copy)\
                    .then_inc(moved, 1)

            def side_xt(phase, layer, n, m):
                side_filled(phase, layer, n, "xt")
                nc.scalar.activation(s_xt[:, :], side[:, :], ACT.Copy).then_inc(s_xt_ready, 1)

            def side_qkv(phase, layer, n, m, t):
                side_filled(phase, layer, n, f"qkv{t}")
                nc.scalar.activation(side_qkv_of(phase, m)[:, t, 0:3 * C], qkv_bank(phase, t)[:, 0:3 * C], ACT.Copy)\
                    .then_inc(s_qkv_ready, 1)

            def side_ot(phase, layer, n, m):
                side_filled(phase, layer, n, "ot")
                nc.scalar.activation(s_ot[:, :], side[:, :], ACT.Copy).then_inc(s_ot_ready, 1)

            def a_exp(m, g):
                act.wait_ge(a_s_ready, m * 2 + (g + 1))
                rows = slice(g * 2 * AH, (g + 1) * 2 * AH)
                nc.scalar.activation(a_p[:, rows, :], a_s[:, rows, :], ACT.Exp, scale=A_SCALE).then_inc(a_p_ready, 1)

            def b_exp(m):
                act.wait_ge(b_q_ready, m + 1)
                nc.scalar.activation(b_e[:, :, :], b_q[:, :, :], ACT.Exp).then_inc(b_e_ready, 1)
                for k in range(2):
                    rows = slice(k * BUCKET, (k + 1) * BUCKET)
                    nc.scalar.activation(b_k[rows, k, :, :], s_qkv[rows, :, C:2 * C], ACT.Exp).then_inc(b_k_ready, 1)

            def b_qt_step(phase, n, m):
                side_filled(phase, "b", n, "qt")
                nc.scalar.activation(b_qt[:, :], side[:, :], ACT.Copy).then_inc(b_qt_ready, 1)

            def side_slot(phase, layer, n, m, u):
                if not layer:
                    return
                if u == SIDE_XT:
                    side_xt(phase, layer, n, m)
                if u in SIDE_QKV:
                    side_qkv(phase, layer, n, m, SIDE_QKV.index(u))
                if layer == "a":
                    if u in A_EXP:
                        a_exp(m, A_EXP.index(u))
                    if u == A_OT:
                        side_ot(phase, "a", n, m)
                else:
                    if u == B_EXP:
                        b_exp(m)
                    if u == B_QT:
                        b_qt_step(phase, n, m)
                    if u == B_OT:
                        side_ot(phase, "b", n, m)

            def period(phase, n, layer, m):
                for u in range(UNITS):
                    if phase == "first" and u == 1:
                        side_ot("start", "a", 1, 1)
                    side_slot(phase, layer, n, m, u - 1)
                    if u in MISC_SLOTS and runs(phase, MISC_SLOTS[u]):
                        misc_step(phase, n, MISC_SLOTS[u])
                    move_step(n, u)
                    if u + 2 < UNITS:
                        exp_step(n, u + 2)
                    elif phase != "last":
                        exp_step(n + 1, u + 2 - UNITS)

            def tail():
                misc_step("tail", PERIODS, "scale3-")

            side_xt("start", "a", 0, 0)
            for t in range(NT):
                side_qkv("start", "a", 0, 0, t)
            weights_hi()
            a_exp(0, 0)
            a_exp(0, 1)
            side_xt("start", "a", 1, 1)
            for t in range(NT):
                side_qkv("start", "a", 1, 1, t)
            side_ot("start", "a", 0, 0)
            a_exp(1, 0)
            a_exp(1, 1)
            for task in ORDER["start"]:
                misc_step("start", -1, task)
            exp_step(0, 0)
            exp_step(0, 1)
            period("first", 0, "a", A_AHEAD)
            with act.Fori(1, A_PERIODS) as n:
                period("loop", n, "a", n + A_AHEAD)
            with act.Fori(0, B) as m:
                period("loop", m + B_FROM, "b", m)
            period("loop", LAST - 1, None, 0)
            period("last", LAST, None, 0)
            tail()

        F_LINKS = 5
        A_LINKS = 4
        START_LINKS = A_LINKS + 2
        B_LINKS = 9

        @block.vector
        def _(dve):
            dve.sem_inc(a_prod_used, 2)
            dve.sem_inc(b_x_done, 1)
            def split_weights():
                dve.wait_ge(w_hi_done, 3)
                nc.vector.scalar_tensor_tensor(out=w_lo[:, 0:FC], in0=raw_wq, scalar=F_SCALE,
                                               in1=w_hi[:, 0:FC].bitcast(fp32), op0=ALU.mult, op1=ALU.subtract)\
                    .then_inc(w_lo_done, 1)
                nc.vector.tensor_tensor(w_lo[:, FC:3 * FC], raw_wkv, w_hi[:, FC:3 * FC].bitcast(fp32),
                                        ALU.subtract).then_inc(w_lo_done, 1)
                nc.vector.tensor_tensor(ws_lo[:, :], raw_ws[:, :], ws_hi[:, :].bitcast(fp32), ALU.subtract)\
                    .then_inc(w_lo_done, 1)

            class Links:

                def __init__(self, sem, base, count):
                    self.sem, self.base, self.count, self.k = sem, base, count, 0

                def link(self, ins):
                    self.k += 1
                    ins.then_inc(self.sem, 1)
                    dve.wait_ge(self.sem, self.base + self.k)

                def end(self):
                    assert self.k == self.count, (self.k, self.count)

            def side_filled(phase, layer, n, task):
                dve.wait_ge(side_full, side_number(phase, layer, n, task) + 1)

            def norm_step(links, slot, stats, mv, var, ready):
                for t in range(NT):
                    last = nc.vector.bn_stats(
                        stats[:, t, :], x_all[:, bass.ds(slot, 1), t * C:(t + 1) * C].rearrange("p o c -> p (o c)"))
                links.link(last)
                dve.nop(nofuse=True)
                for t in range(NT):
                    last = nc.vector.bn_aggr(mv[:, t, :], stats[:, t, :])
                links.link(last)
                nc.vector.tensor_scalar(var[:, :], mv[:, :, 1], EPS, None, ALU.add).then_inc(ready, 1)

            def xn_step(slot, mv, rstd, xn, ready):
                for t in range(NT):
                    last = nc.vector.tensor_scalar(
                        xn[:, t, :], x_all[:, bass.ds(slot, 1), t * C:(t + 1) * C].rearrange("p o c -> p (o c)"),
                        mv[:, t, 0:1], rstd[:, t:t + 1], ALU.subtract, ALU.mult)
                last.then_inc(ready, 1)

            def f_norm(links, n, first):
                if first:
                    dve.wait_ge(a_x_done, n + 1)
                else:
                    dve.wait_ge(a_x_done, B)
                    dve.wait_ge(b_x_done, n - (B - 2))
                norm_step(links, n, f_stats, f_mv, f_var, f_var_ready)

            def f_xn_step(n):
                dve.wait_ge(f_rstd_ready, n + 1)
                xn_step(n, f_mv, f_rstd, f_xn, f_xn_ready)

            def lower_parts(n, task):
                s, name = seq_of(n, task)
                if name == "xt":
                    dve.wait_ge(xt_hi_ready, s + 1)
                    nc.vector.tensor_tensor(xt_lo[:, :], misc[:, :], xt_hi[:, :].bitcast(fp32), ALU.subtract)\
                        .then_inc(xt_lo_ready, 1)
                    return
                if name[0] not in "qk":
                    return
                p = int(name[1])
                dve.wait_ge(qk_hi_ready, s * 2 * NP + (2 * p + (name[0] == "k") + 1))
                for a, (own, other) in enumerate(((LOW, HIGH), (HIGH, LOW))):
                    if name[0] == "q":
                        last = nc.vector.tensor_tensor(q_both[other, p % 2, a, :], misc[own, :],
                                                       q_both[own, p % 2, a, :].bitcast(fp32), ALU.subtract)
                    else:
                        last = nc.vector.tensor_tensor(k_cross[own, p % 2, a, :], misc[own, :],
                                                       k_hi[own, p % 2, :].bitcast(fp32), ALU.subtract)
                last.then_inc(qk_lo_ready, 1)

            def gate_step(links, n, part):
                if part == 0:
                    dve.wait_ge(gate_exp_ready, n + 1)
                    links.link(nc.vector.tensor_scalar(g_den[:, :, :], g_exp[:, :, :], 1.0, None, ALU.add))
                    links.link(nc.vector.reciprocal(g_sig[:, :, :], g_den[:, :, :]))
                    mine = g_sig[:, :, :].rearrange("p t (h o) -> p t h o", o=1).to_broadcast([P, NT, FH, FH])
                    other = g_sig[:, :, :].rearrange("p t (o h) -> p t o h", o=1).to_broadcast([P, NT, FH, FH])
                    nc.vector.tensor_tensor(g_gt[:, :, :, :], other, mine, ALU.is_gt)
                    nc.vector.tensor_tensor(g_ge[:, :, :, :], other, mine, ALU.is_ge).then_inc(g_compared, 1)
                if part == 1:
                    dve.wait_ge(g_marks_ready, n + 1)
                    links.link(nc.vector.reduce_sum(g_rank[:, :, :], g_ge[:, :, :, :], AX.X))
                    nc.vector.scalar_tensor_tensor(out=gate[:, :, :], in0=g_rank[:, :, :], scalar=TOPK - 0.5,
                                                   in1=g_sig[:, :, :], op0=ALU.is_lt, op1=ALU.mult)\
                        .then_inc(gate_ready, 1)

            def max_step(n, u):
                dve.wait_ge(scores_ready, n * UNITS + (u + 1))
                nc.vector.tensor_reduce(neg_max[:, u:u + 1], scores[u % 3][:, :], AX.X, ALU.max, negate=True)\
                    .then_inc(max_ready, 1)

            def recip_step(n, p):
                dve.wait_ge(exp_done, n * UNITS + PAIR * (p + 1))
                nc.vector.reciprocal(recip[:, :, :], row_sum[:, PAIR * p:PAIR * (p + 1)]
                                     .rearrange("p (a t) -> p a t", a=2)).then_inc(recip_ready, 1)

            def out_step(n, p):
                dve.wait_ge(heads_ready, n * NP + (p + 1))
                dve.wait_ge(scale_t_ready, n * NP + (p + 1))
                nc.vector.tensor_tensor(out_t[:, p, :], heads_out[:, :], scale_t[:, :], ALU.mult)\
                    .then_inc(heads_scaled, 1)

            def add_step(dst, src, bank_ap, done):
                nc.vector.tensor_tensor(x_all[:, bass.ds(dst, 1), :].rearrange("p o c -> p (o c)"), bank_ap,
                                        x_all[:, bass.ds(src, 1), :].rearrange("p o c -> p (o c)"), ALU.add)\
                    .then_inc(done, 1)

            def wo_step(phase, layer, n):
                side_filled(phase, layer, n, "wo-")
                add_step(n - 1, n - 1, side[:, :], f_x_done)

            def a_norm(links, m, wait_load):
                if wait_load:
                    dve.wait_ge(loaded_first if m == 0 else loaded_x, 16)
                norm_step(links, m, s_stats, s_mv, s_var, s_var_ready)

            def side_xn(layer, m):
                dve.wait_ge(s_rstd_ready, side_seq(layer, m) + 1)
                xn_step(m, s_mv, s_rstd, s_xn, s_xn_ready)

            def own_product(links, kind, m, t):
                k = m * 2 + kind
                if k:
                    dve.wait_ge(a_own_summed, k)
                if kind == 0:
                    dve.wait_ge(s_qkv_ready, m * NT + (t + 1))
                    links.link(a_scores_product(nc.vector, "start", m, a_own[:, :], t))
                else:
                    dve.wait_ge(a_p_ready, m * 2 + 2)
                    links.link(a_values_product(nc.vector, "start", m, a_own[:, :], t))

            def a_scores_sum(phase, m, t, half=None):
                heads = slice(0, AH) if half is None else slice(half * AH // 2, (half + 1) * AH // 2)
                own = t >= pool_tiles(phase)
                if not own and half != 1:
                    dve.wait_ge(a_prod_ready, pool_products(phase, m) + (t + 1))
                src = a_own[:, :] if own else a_prod[:, t % 2, :]
                ins = nc.vector.reduce_sum(a_s[:, t * AH:(t + 1) * AH, :][:, heads, :],
                                           src.rearrange("p (h t d) -> p h t d", h=AH, t=AH)[:, heads, :, :], AX.X)
                if half != 0:
                    ins.then_inc(a_own_summed if own else a_prod_used, 1)

            def a_softmax(phase, links, m, g):
                dve.wait_ge(a_prod_used, pool_products(phase, m) + (min(2 * g + 2, pool_tiles(phase)) + 2))
                if g == 1 and phase == "start":
                    dve.wait_ge(a_own_summed, m * 2 + 1)
                rows = slice(g * 2 * AH, (g + 1) * 2 * AH)
                links.link(nc.vector.reduce_max(a_max[:, rows], a_s[:, rows, :], AX.X))
                nc.vector.tensor_tensor(a_s[:, rows, :], a_s[:, rows, :],
                                        a_max[:, rows].rearrange("p (h o) -> p h o", o=1)
                                        .to_broadcast([P, 2 * AH, AH]), ALU.subtract).then_inc(a_s_ready, 1)

            def a_sums(m, g):
                dve.wait_ge(a_p_ready, m * 2 + (g + 1))
                rows = slice(g * 2 * AH, (g + 1) * 2 * AH)
                nc.vector.reduce_sum(a_sum[:, rows], a_p[:, rows, :], AX.X).then_inc(a_sum_ready, 1)

            def a_reciprocal(m):
                dve.wait_ge(a_sum_ready, m * 2 + 2)
                nc.vector.reciprocal(a_rec[:, :], a_sum[:, :]).then_inc(a_rec_ready, 1)

            def a_values_sum(phase, m, t, half=None):
                heads = slice(0, AH) if half is None else slice(half * AH // 2, (half + 1) * AH // 2)
                own = t >= pool_tiles(phase)
                k = pool_tiles(phase) + t
                if not own and half != 1:
                    dve.wait_ge(a_prod_ready, pool_products(phase, m) + (k + 1))
                src = a_own[:, :] if own else a_prod[:, k % 2, :]
                ins = nc.vector.reduce_sum(s_o[:, t, :].rearrange("p (h d) -> p h d", h=AH)[:, heads, :],
                                           src.rearrange("p (h d t) -> p h d t", h=AH, d=AD)[:, heads, :, :], AX.X)
                if half != 0:
                    ins.then_inc(a_own_summed if own else a_prod_used, 1)

            def a_normalise(phase, m):
                dve.wait_ge(a_prod_used, pool_products(phase, m) + (2 * pool_tiles(phase) + 2))
                if phase == "start":
                    dve.wait_ge(a_own_summed, m * 2 + 2)
                dve.wait_ge(a_rec_ready, m + 1)
                o = s_o[:, :, :].rearrange("p t (h d) -> p (t h) d", d=AD)
                nc.vector.tensor_tensor(o, o, a_rec[:, :].rearrange("p (h o) -> p h o", o=1)
                                        .to_broadcast([P, NT * AH, AD]), ALU.mult).then_inc(s_o_ready, 1)

            def side_add(phase, layer, n, m):
                side_filled(phase, layer, n, "fc")
                if layer == "a":
                    add_step(m, m, side[:, :], a_x_done)
                else:
                    add_step(m + B, m, side[:, :], b_x_done)

            def b_norm(links, m):
                dve.wait_ge(f_x_done, m + 1)
                norm_step(links, m, s_stats, s_mv, s_var, s_var_ready)

            def b_query_max(links, m):
                dve.wait_ge(s_qkv_ready, (m + (B + 1)) * NT)
                q = s_qkv[:, :, 0:C].rearrange("p t (h d) -> p t h d", d=AD)
                top = a_max[:, :].rearrange("p (t h) -> p t h", t=NT)
                links.link(nc.vector.reduce_max(top, q, AX.X))
                nc.vector.tensor_tensor(b_q[:, :, :].rearrange("p t (h d) -> p t h d", d=AD), q,
                                        top.rearrange("p t (h o) -> p t h o", o=1).to_broadcast([P, NT, AH, AD]),
                                        ALU.subtract).then_inc(b_q_ready, 1)

            def b_query_softmax(links, m):
                dve.wait_ge(b_e_ready, m + 1)
                e = b_e[:, :, :].rearrange("p t (h d) -> p (t h) d", d=AD)
                links.link(nc.vector.reduce_sum(a_sum[:, :], e, AX.X))
                links.link(nc.vector.reciprocal(a_rec[:, :], a_sum[:, :]))
                nc.vector.scalar_tensor_tensor(
                    out=b_q[:, :, :].rearrange("p t (h d) -> p (t h) d", d=AD), in0=e, scalar=A_SCALE,
                    in1=a_rec[:, :].rearrange("p (h o) -> p h o", o=1).to_broadcast([P, NT * AH, AD]),
                    op0=ALU.mult, op1=ALU.mult).then_inc(b_qn_ready, 1)

            def b_sums(phase, n, m, g):
                side_filled(phase, "b", n, f"ctx{g}")
                for k in range(3 * g, min(3 * g + 3, NB - 1)):
                    j = (k - 3 * g) * CW
                    if k == 0:
                        ins = nc.vector.tensor_copy(b_cum[:, 1, :], side[:, 0:CW])
                    else:
                        dve.wait_ge(b_cum_ready, m * (NB - 1) + k)
                        ins = nc.vector.tensor_tensor(b_cum[:, k + 1, :], side[:, j:j + CW], b_cum[:, k, :], ALU.add)
                    ins.then_inc(b_cum_ready, 1)

            def b_attend(phase, links, n, m, g):
                side_filled(phase, "b", n, f"att{g}")
                a = side[:, 0:2 * CW].rearrange("p (t c) -> p t c", t=2)
                links.link(nc.vector.tensor_scalar(b_den[:, :, :], a[:, :, C:CW], 1e-6, None, ALU.max))
                links.link(nc.vector.reciprocal(b_inv[:, :, :], b_den[:, :, :]))
                nc.vector.tensor_tensor(
                    s_o[:, 2 * g:2 * g + 2, :].rearrange("p t (h d) -> p t h d", d=AD),
                    a[:, :, 0:C].rearrange("p t (h d) -> p t h d", d=AD),
                    b_inv[:, :, :].rearrange("p t (h o) -> p t h o", o=1).to_broadcast([P, 2, AH, AD]),
                    ALU.mult).then_inc(s_o_ready, 1)

            def side_slot(phase, layer, links, n, m, u):
                if layer == "a":
                    if u == SIDE_NORM:
                        a_norm(links, m, False)
                    if u == SIDE_XN:
                        side_xn("a", m)
                    for k in range(2 * NT):
                        if u == A_SCORES_SLOTS[k]:
                            a_scores_sum(phase, m, k // 2, k % 2)
                    if u in A_SOFTMAX:
                        a_softmax(phase, links, m, A_SOFTMAX.index(u))
                    if u in A_SUMS:
                        a_sums(m, A_SUMS.index(u))
                    if u == A_RECIP:
                        a_reciprocal(m)
                    for k in range(2 * NT):
                        if u == A_VALUES_SLOTS[k]:
                            a_values_sum(phase, m, k // 2, k % 2)
                    if u == A_NORMALISE:
                        a_normalise(phase, m)
                    if u == A_ADD:
                        side_add(phase, "a", n, m)
                if layer == "b":
                    if u == SIDE_NORM:
                        b_norm(links, m)
                    if u == SIDE_XN:
                        side_xn("b", m)
                    if u == B_MAX:
                        b_query_max(links, m)
                    if u == B_SOFTMAX:
                        b_query_softmax(links, m)
                    if u in B_SUM:
                        b_sums(phase, n, m, B_SUM.index(u))
                    if u in B_OUT:
                        b_attend(phase, links, n, m, B_OUT.index(u))
                    if u == B_ADD:
                        side_add(phase, "b", n, m)

            def period(phase, n, layer, m):
                links = Links(f_chain, n * F_LINKS + 2, F_LINKS if phase != "last" else F_LINKS - 2)
                a_more = A_AHEAD * (START_LINKS - A_LINKS)
                side_links = Links(s_chain, m * A_LINKS + a_more, A_LINKS) if layer == "a" else \
                    Links(s_chain, m * B_LINKS + (B * A_LINKS + a_more), B_LINKS)
                for u in range(UNITS):
                    if u in RECIP_SLOTS and runs(phase, RECIP_SLOTS[u]):
                        s, p = seq_of(n, RECIP_SLOTS[u])
                        recip_step(s, int(p))
                    if u + 2 < UNITS:
                        max_step(n, u + 2)
                    elif phase != "last":
                        max_step(n + 1, u + 2 - UNITS)
                    if u in MISC_SLOTS and runs(phase, MISC_SLOTS[u]):
                        lower_parts(n, MISC_SLOTS[u])
                    if u in GATE_SLOTS:
                        gate_step(links, n, GATE_SLOTS.index(u))
                    if u == WO_ADD and phase != "first":
                        wo_step(phase, layer, n)
                    if u in OUT_SLOTS and runs(phase, OUT_SLOTS[u]):
                        s, p = seq_of(n, OUT_SLOTS[u])
                        out_step(s, int(p))
                    if phase != "last":
                        if u == NORM_SLOT:
                            f_norm(links, n + 1, None if layer == "b" else n + 1 < B)
                        if u == XN_SLOT:
                            f_xn_step(n + 1)
                    if phase == "first" and u == 2:
                        side_add("start", "a", 1, 1)
                    side_slot(phase, layer, side_links, n, m, u)
                links.end()
                if layer:
                    side_links.end()

            def tail():
                recip_step(LAST, NP - 1)
                out_step(LAST, NP - 1)
                wo_step("tail", None, PERIODS)

            def start():
                links = Links(s_chain, 0, A_AHEAD * START_LINKS)
                f_links = Links(f_chain, 0, 2)

                a_norm(links, 0, True)
                nc.vector.memset(s_qkv[:, :, 3 * C:3 * C + AH], 1.0).then_inc(ones_done, 1)
                nc.vector.memset(b_k[:, :, :, :], 0.0).then_inc(ones_done, 1)
                side_xn("a", 0)
                dve.wait_ge(w_turned, 1)
                nc.vector.tensor_copy(a_w[:, 0:2 * C], scores[0][:, 0:2 * C]).then_inc(w_copied, 1)
                nc.vector.tensor_copy(a_w[:, 2 * C:3 * C].rearrange("p (d t) -> p d t", d=AD),
                                      scores[0][:, 2 * C:3 * C].rearrange("p (t d) -> p d t", d=AD))\
                    .then_inc(w_copied, 1)
                nc.vector.tensor_copy(a_fc[:, :], scores[0][:, 3 * C:4 * C]).then_inc(w_copied, 1)
                nc.vector.tensor_copy(b_w[:, :], scores[1][:, 0:3 * C]).then_inc(w_copied, 1)
                nc.vector.tensor_copy(b_out[:, :], scores[1][:, 3 * C:4 * C]).then_inc(w_copied, 1)
                own_product(links, 0, 0, 3)
                a_scores_sum("start", 0, 3)
                a_scores_sum("start", 0, 0)
                dve.wait_ge(s_xn_ready, 1)
                a_norm(links, 1, True)
                a_scores_sum("start", 0, 1)
                a_softmax("start", links, 0, 0)
                dve.wait_ge(s_xt_ready, 1)
                side_xn("a", 1)
                split_weights()
                a_scores_sum("start", 0, 2)
                a_softmax("start", links, 0, 1)
                own_product(links, 1, 0, 3)
                a_values_sum("start", 0, 3)
                a_values_sum("start", 0, 0)
                a_sums(0, 0)
                a_sums(0, 1)
                a_values_sum("start", 0, 1)
                a_reciprocal(0)
                a_values_sum("start", 0, 2)
                a_normalise("start", 0)
                own_product(links, 0, 1, 3)
                a_scores_sum("start", 1, 3)
                a_scores_sum("start", 1, 0)
                side_add("start", "a", 0, 0)
                dve.wait_ge(masks_done, 4)
                f_norm(f_links, 0, True)
                a_scores_sum("start", 1, 1)
                a_softmax("start", links, 1, 0)
                f_xn_step(0)
                a_scores_sum("start", 1, 2)
                a_softmax("start", links, 1, 1)
                lower_parts(-1, "xt+")
                own_product(links, 1, 1, 3)
                lower_parts(-1, "q0+")
                a_values_sum("start", 1, 3)
                a_values_sum("start", 1, 0)
                lower_parts(-1, "k0+")
                a_sums(1, 0)
                a_sums(1, 1)
                max_step(0, 0)
                a_values_sum("start", 1, 1)
                max_step(0, 1)
                a_reciprocal(1)
                a_values_sum("start", 1, 2)
                a_normalise("start", 1)
                links.end()
                f_links.end()

            start()
            period("first", 0, "a", A_AHEAD)
            with dve.Fori(1, A_PERIODS) as n:
                period("loop", n, "a", n + A_AHEAD)
            with dve.Fori(0, B) as m:
                period("loop", m + B_FROM, "b", m)
            period("loop", LAST - 1, None, 0)
            period("last", LAST, None, 0)
            tail()

        @block.tensor
        def _(pe):
            def misc_claim(phase, n, task):
                event = misc_before(phase, n, task)
                if event:
                    pe.wait_ge(*event)

            def side_claim(phase, layer, n, m, task):
                if phase == "start":
                    at = START_SIDE.index((m, task))
                    if at:
                        pe.wait_ge(*side_read("a", n, *START_SIDE[at - 1]))
                    return
                order = [t for t in SIDE[layer] if t != "wo-" or phase != "first"]
                at = order.index(task)
                if at:
                    pe.wait_ge(*side_read(layer, n, m, order[at - 1]))
                elif task == "wo-":
                    pe.wait_ge(b_x_done, B + 1)
                    pe.wait_ge(f_x_done, n - 1)

            def split_product(dst, l_hi, l_lo, r_hi, r_lo):
                nc.tensor.matmul(dst, l_hi, r_lo, start=True, stop=False)
                nc.tensor.matmul(dst, l_lo, r_hi, start=False, stop=False)
                return nc.tensor.matmul(dst, l_hi, r_hi, start=False, stop=True)

            def misc_step(phase, n, task):
                misc_claim(phase, n, task)
                s, name = seq_of(n, task)
                if name == "xt":
                    pe.wait_ge(f_xn_ready, s + 1)
                    for t in range(NT):
                        last = nc.tensor.transpose(tile_of(misc, t), f_xn[:, t, :], ident[:, :])
                if name == "logits":
                    for t in range(NT):
                        last = split_product(misc[:, t * FH:(t + 1) * FH], tile_of(xt_hi, t), tile_of(xt_lo, t),
                                             ws_hi[:, :], ws_lo[:, :])
                if name == "gate_t":
                    pe.wait_ge(gate_ready, s + 1)
                    for t in range(NT):
                        last = nc.tensor.transpose(misc[0:FH, t * P:(t + 1) * P], gate[:, t, :], ident[:, :])
                if name[:5] == "scale":
                    pe.wait_ge(scale_ready, s * NP + (int(name[5]) + 1))
                    for t in range(NT):
                        last = nc.tensor.transpose(tile_of(misc, t),
                                                   scale_w[:, t, :, :].rearrange("p a d -> p (a d)"), ident[:, :])
                if name[0] == "v":
                    t = int(name[1])
                    last = split_product(misc[:, :], tile_of(xt_hi, t), tile_of(xt_lo, t),
                                         w_hi[:, 2 * FC:3 * FC], w_lo[:, 2 * FC:3 * FC])
                if name[0] in "qk":
                    if name == "q0":
                        pe.wait_ge(xt_lo_ready, s + 1)
                    c = (FC if name[0] == "k" else 0) + int(name[1]) * P
                    last = split_product(misc[:, :], w_hi[:, c:c + P], w_lo[:, c:c + P], xt_hi[:, :], xt_lo[:, :])
                last.then_inc(misc_full, 1)

            def scores_step(n, u):
                h, t = u // NT, u % NT
                p, r = h // 2, (h % 2) * FD
                if u % PAIR == 0:
                    pe.wait_ge(qk_lo_ready, n * 2 * NP + (2 * p + 2))
                    pe.wait_ge(k_cross_hi_ready, n * NP + (p + 1))
                q = slice(t * P, (t + 1) * P)
                dst = scores[u % 3][:, :]
                nc.tensor.matmul(dst, q_both[:, p % 2, h % 2, q], k_cross[:, p % 2, h % 2, :], start=True, stop=False)
                nc.tensor.matmul(dst, q_both[r:r + FD, p % 2, h % 2, q], k_hi[r:r + FD, p % 2, :],
                                 start=False, stop=True).then_inc(scores_ready, 1)

            def turn_step(phase, n, u):
                pe.wait_ge(exp_done, n * UNITS + (u + 1))
                for c in range(NT):
                    last = nc.tensor.transpose(tile_of(turned[u % 2], c), probs[:, u % 4, c * P:(c + 1) * P],
                                               ident[:, :])
                last.then_inc(turned_ready, 1)

            def pv_step(phase, n, pair, c):
                s, p = seq_of(n, pair)
                p = int(p)
                if c == 0:
                    if phase == "tail":
                        pe.wait_ge(moved, s * UNITS + PAIR * (p + 1))
                    if p or phase != "first":
                        pe.wait_ge(heads_scaled, s * NP + p)
                if p == 0:
                    pe.wait_ge(v_ready, s * NT + (c + 1))
                for a in range(2):
                    h = 2 * p + a
                    last = nc.tensor.matmul(heads_out[a * FD:(a + 1) * FD, :], v_sb[:, c, h * FD:(h + 1) * FD],
                                            probs_t[:, h % 4, c, :], start=(c == 0), stop=(c == NT - 1))
                if c == NT - 1:
                    last.then_inc(heads_ready, 1)

            def wo_step(phase, layer, n, m, t):
                if t == 0:
                    side_claim(phase, layer, n, m, "wo-")
                    pe.wait_ge(gate_t_ready, n)
                    pe.wait_ge(heads_scaled, n * NP)
                nc.tensor.matmul(tile_of(side, t), gate_t[:, t * P:(t + 1) * P], bo[:, :], start=True, stop=False)
                for p in range(NP):
                    last = nc.tensor.matmul(tile_of(side, t), out_t[:, p, t * P:(t + 1) * P], wo[:, p, :],
                                            start=False, stop=(p == NP - 1))
                if t == NT - 1:
                    last.then_inc(side_full, 1)

            def side_turn(phase, layer, n, m, task, ready, value, src):
                side_claim(phase, layer, n, m, task)
                pe.wait_ge(ready, value)
                for t in range(NT):
                    last = nc.tensor.transpose(tile_of(side, t), src[:, t, :], ident[:, :])
                last.then_inc(side_full, 1)

            def side_xt(phase, layer, n, m):
                side_turn(phase, layer, n, m, "xt", s_xn_ready, side_seq(layer, m) + 1, s_xn)

            def side_qkv(phase, layer, n, m, t):
                if t == 0 or phase != "start":
                    side_claim(phase, layer, n, m, f"qkv{t}")
                if t == 0:
                    pe.wait_ge(s_xt_ready, side_seq(layer, m) + 1)
                w = a_w if layer == "a" else b_w
                nc.tensor.matmul(qkv_bank(phase, t)[:, 0:3 * C], tile_of(s_xt, t), w[:, :], start=True, stop=True)\
                    .then_inc(side_full, 1)

            def side_ot(phase, layer, n, m):
                side_turn(phase, layer, n, m, "ot", s_o_ready,
                          outputs_before(layer, m) + (1 if layer == "a" else 2), s_o)

            def side_fc(phase, layer, n, m):
                side_claim(phase, layer, n, m, "fc")
                pe.wait_ge(s_ot_ready, side_seq(layer, m) + 1)
                w = a_fc if layer == "a" else b_out
                for t in range(NT):
                    last = nc.tensor.matmul(tile_of(side, t), tile_of(s_ot, t), w[:, :], start=True, stop=True)
                last.then_inc(side_full, 1)

            def b_context(phase, n, m, g):
                side_claim(phase, "b", n, m, f"ctx{g}")
                if g == 0:
                    pe.wait_ge(b_k_ready, m * 2 + 2)
                for k in range(3 * g, min(3 * g + 3, NB - 1)):
                    j, t = (k - 3 * g) * CW, k // 2
                    last = nc.tensor.matmul(side[:, j:j + CW], b_k[:, k % 2, t, :],
                                            s_qkv[:, t, 2 * C:2 * C + CW], start=True, stop=True)
                last.then_inc(side_full, 1)

            def b_attend(phase, n, m, g):
                side_claim(phase, "b", n, m, f"att{g}")
                if g == 0:
                    pe.wait_ge(b_qt_ready, m + 1)
                pe.wait_ge(b_ctx_ready, m * (NB - 1) + (3 if g == 0 else NB - 1))
                for k in range(4 * g, 4 * g + 4):
                    r, j = (k % 2) * BUCKET, (k // 2 - 2 * g) * CW
                    last = nc.tensor.matmul(side[r:r + BUCKET, j:j + CW], b_qt[:, k * BUCKET:(k + 1) * BUCKET],
                                            b_ctx[:, k, :], start=True, stop=True)
                last.then_inc(side_full, 1)

            def side_slot(phase, layer, n, m, u):
                if not layer:
                    return
                if u == SIDE_XT:
                    side_xt(phase, layer, n, m)
                if u in SIDE_QKV:
                    side_qkv(phase, layer, n, m, SIDE_QKV.index(u))
                if layer == "a":
                    if u == A_OT:
                        side_ot(phase, "a", n, m)
                    if u == A_FC:
                        side_fc(phase, "a", n, m)
                if layer == "b":
                    if u == B_QT:
                        side_turn(phase, "b", n, m, "qt", b_qn_ready, m + 1, b_q)
                    if u in B_CTX:
                        b_context(phase, n, m, B_CTX.index(u))
                    if u in B_ATT:
                        b_attend(phase, n, m, B_ATT.index(u))
                    if u == B_OT:
                        side_ot(phase, "b", n, m)
                    if u == B_FC:
                        side_fc(phase, "b", n, m)

            def period(phase, n, layer, m):
                for u in range(UNITS):
                    if u + 2 < UNITS:
                        scores_step(n, u + 2)
                    if u in MISC_SLOTS and runs(phase, MISC_SLOTS[u]):
                        misc_step(phase, n, MISC_SLOTS[u])
                    turn_step(phase, n, u)
                    if u + 2 >= UNITS and phase != "last":
                        scores_step(n + 1, u + 2 - UNITS)
                    if u in WO_SLOTS and phase != "first":
                        for t in WO_SLOTS[u]:
                            wo_step(phase, layer, n, m, t)
                    if phase == "first" and u == 0:
                        side_ot("start", "a", 1, 1)
                    if phase == "first" and u == 1:
                        side_fc("start", "a", 1, 1)
                    side_slot(phase, layer, n, m, u)
                    if u in PV_SLOTS and runs(phase, PV_SLOTS[u][0]):
                        pv_step(phase, n, *PV_SLOTS[u])

            def tail():
                for c in range(NT):
                    pv_step("tail", PERIODS, "3-", c)
                misc_step("tail", PERIODS, "scale3-")
                for t in range(NT):
                    wo_step("tail", None, PERIODS, 0, t)

            pe.wait_ge(ident_done, 1)
            side_xt("start", "a", 0, 0)
            pe.wait_ge(loaded_w, 6 * 16)
            for k in range(8):
                last = nc.tensor.transpose(tile_of(scores[k // 4], k % 4), raw_sq[:, k, :], ident[:, :])
            last.then_inc(w_turned, 1)
            pe.wait_ge(w_copied, 2)
            for t in range(NT):
                side_qkv("start", "a", 0, 0, t)
            side_xt("start", "a", 1, 1)
            for t in range(NT):
                side_qkv("start", "a", 1, 1, t)
            pe.wait_ge(w_copied, 5)
            side_ot("start", "a", 0, 0)
            side_fc("start", "a", 0, 0)
            pe.wait_ge(w_lo_done, 3)
            for task in ORDER["start"]:
                misc_step("start", -1, task)
            scores_step(0, 0)
            scores_step(0, 1)
            period("first", 0, "a", A_AHEAD)
            with pe.Fori(1, A_PERIODS) as n:
                period("loop", n, "a", n + A_AHEAD)
            with pe.Fori(0, B) as m:
                period("loop", m + B_FROM, "b", m)
            period("loop", LAST - 1, None, 0)
            period("last", LAST, None, 0)
            tail()


_INS = ['L0_attn_a_x', 'L0_attn_a_Wq', 'L0_attn_a_Wk', 'L0_attn_a_Wv', 'L0_attn_a_Wfc', 'L0_attn_b_W_qkv',
        'L0_attn_b_W_out', 'L0_ffn_Wq', 'L0_ffn_Wkv', 'L0_ffn_Ws', 'L0_ffn_Wo', 'L0_ffn_bo']
_OUTS = [((8, 512, 128), 'float32')]


def kernel(**inputs):
    import numpy as _np
    import concourse.bacc as _bacc
    from concourse import mybir as _mybir
    from concourse.bass_utils import run_bass_kernel_spmd as _run

    nc = _bacc.Bacc("TRN2", target_bir_lowering=False, num_devices=1)
    arrays, args = {}, []
    for name in _INS:
        a = _np.ascontiguousarray(inputs[name])
        arrays[f"in_{name}_dram"] = a
        args.append(nc.dram_tensor(f"in_{name}_dram", a.shape, _mybir.dt.from_np(a.dtype), kind="ExternalInput").ap())
    for i, (shape, dtype) in enumerate(_OUTS):
        dt = _mybir.dt.from_np(_np.dtype(dtype))
        args.append(nc.dram_tensor(f"out_{i}_dram", shape, dt, kind="ExternalOutput").ap())
    bass_hybrid_attention_ffn_kernel(nc, *args)
    r = _run(nc, [arrays], core_ids=[0])
    got = tuple(r.results[0][f"out_{i}_dram"] for i in range(len(_OUTS)))
    return got[0]
```
